# Optimizing a Trainium2 kernel written in Bass

```python
import numpy as np
import jax
import jax.numpy as jnp

def _softmax(x, axis=-1):
    return jax.nn.softmax(x, axis=axis)

def _gelu(x):
    return jax.nn.gelu(x, approximate=True)

def _silu(x):
    return jax.nn.silu(x)

def _sigmoid(x):
    return jax.nn.sigmoid(x)

def _layernorm(x, axis=-1, eps=1e-05):
    m = jnp.mean(x, axis=axis, keepdims=True)
    v = jnp.var(x, axis=axis, keepdims=True)
    return (x - m) / jnp.sqrt(v + eps)

def _scatter_add(tgt, idx, src, axis=0):
    return tgt.at[idx].add(src)

def _segment_sum(src, seg, n):
    return jax.ops.segment_sum(src, seg, n)
kernel_name = 'mk_seq_preln_d1_jaxref_r4_afc477'

def setup_inputs(seed: int=0):
    np.random.seed(seed)
    _w = jnp.asarray

    def _L0_attn_setup():
        import jax, jax.numpy as jnp
        import numpy as np
        D_MODEL = 256
        N_LAYERS = 2
        D_STATE = 64
        D_CONV = 4
        EXPAND = 2
        D_INNER = EXPAND * D_MODEL
        HEADDIM = D_STATE
        NHEADS = D_INNER // HEADDIM
        CONV_DIM = D_INNER + 2 * D_STATE
        D_IN_PROJ = 2 * D_INNER + 2 * D_STATE + NHEADS
        EPS = 1e-05

        def _layernorm(x, w, b):
            m = x.mean(-1, keepdims=True)
            v = ((x - m) ** 2).mean(-1, keepdims=True)
            return (x - m) * jax.lax.rsqrt(v + EPS) * w + b

        def _mamba2(u, in_w, conv_w, conv_b, dt_bias, A_log, Dp, rms_w, out_w):
            b, l, _ = u.shape
            zxbcdt = u @ in_w.T
            z, xBC, dt = jnp.split(zxbcdt, [D_INNER, D_INNER + CONV_DIM], axis=-1)
            dt = jax.nn.softplus(dt + dt_bias)
            xBC = jnp.transpose(xBC, (0, 2, 1))
            xBC = jax.lax.conv_general_dilated(xBC, conv_w[:, None, :], (1,), [(D_CONV - 1, 0)], dimension_numbers=('NCH', 'OIH', 'NCH'), feature_group_count=CONV_DIM)
            xBC = jnp.transpose(xBC, (0, 2, 1)) + conv_b
            xBC = jax.nn.silu(xBC)
            xh, Bm, Cm = jnp.split(xBC, [D_INNER, D_INNER + D_STATE], axis=-1)
            xh = xh.reshape(b, l, NHEADS, HEADDIM)
            A = -jnp.exp(A_log)
            dA = jnp.exp(dt * A)

            def step(state, inputs):
                dA_t, dt_t, x_t, B_t, C_t = inputs
                state = dA_t[:, :, None, None] * state + (dt_t[:, :, None] * x_t)[..., None] * B_t[:, None, None, :]
                y_t = jnp.einsum('bhpn,bn->bhp', state, C_t)
                return (state, y_t)
            xs = (jnp.moveaxis(dA, 1, 0), jnp.moveaxis(dt, 1, 0), jnp.moveaxis(xh, 1, 0), jnp.moveaxis(Bm, 1, 0), jnp.moveaxis(Cm, 1, 0))
            init = jnp.zeros((b, NHEADS, HEADDIM, D_STATE), u.dtype)
            _, ys = jax.lax.scan(step, init, xs)
            y = jnp.moveaxis(ys, 0, 1) + Dp[None, None, :, None] * xh
            y = y.reshape(b, l, D_INNER)
            y = y * jax.nn.silu(z)
            y = y * jax.lax.rsqrt(jnp.mean(y * y, -1, keepdims=True) + EPS) * rms_w
            return y @ out_w.T
        key = jax.random.key(seed)
        ks = jax.random.split(key, 8)
        B, L = (2, 1024)
        return {'x': jax.random.normal(ks[0], (B, L, D_MODEL), jnp.float32), 'ln_w': jnp.ones((N_LAYERS, D_MODEL), jnp.float32), 'ln_b': jnp.zeros((N_LAYERS, D_MODEL), jnp.float32), 'in_proj_w': jax.random.normal(ks[1], (N_LAYERS, D_IN_PROJ, D_MODEL), jnp.float32) * D_MODEL ** (-0.5), 'conv_w': jax.random.normal(ks[2], (N_LAYERS, CONV_DIM, D_CONV), jnp.float32) * D_CONV ** (-0.5), 'conv_b': jnp.zeros((N_LAYERS, CONV_DIM), jnp.float32), 'dt_bias': jax.random.normal(ks[3], (N_LAYERS, NHEADS), jnp.float32) * 0.5, 'A_log': jnp.log(jax.random.uniform(ks[4], (N_LAYERS, NHEADS), jnp.float32, 1.0, 16.0)), 'D': jnp.ones((N_LAYERS, NHEADS), jnp.float32), 'rms_w': jnp.ones((N_LAYERS, D_INNER), jnp.float32), 'out_proj_w': jax.random.normal(ks[5], (N_LAYERS, D_MODEL, D_INNER), jnp.float32) * D_INNER ** (-0.5)}
    _L0_attn_in = _L0_attn_setup()

    def _L0_ffn_setup():
        import jax, jax.numpy as jnp
        import numpy as np
        GROUP = 16
        EPS = 1e-05

        def _dequant(q, scale):
            w = q.astype(jnp.float32) / 7.5 - 1.0
            return w * jnp.repeat(scale, GROUP, axis=1)

        def _qlora_linear(x, q, scale, bias, la, lb):
            w = _dequant(q, scale)
            base = jnp.einsum('btd,od->bto', x, w) + bias
            lora = jnp.einsum('btr,or->bto', jnp.einsum('btd,rd->btr', x, la), lb)
            return base + lora

        def _layernorm(x, g, b):
            mu = jnp.mean(x, axis=-1, keepdims=True)
            var = jnp.mean(jnp.square(x - mu), axis=-1, keepdims=True)
            return (x - mu) * jax.lax.rsqrt(var + EPS) * g + b
        key = jax.random.key(seed)
        ks = jax.random.split(key, 6)
        D, R, B, T = (256, 32, 8, 1024)
        x = jax.random.normal(ks[0], (B, T, D), dtype=jnp.float32)
        qweights = jax.random.randint(ks[1], (6, D, D), 0, 16, dtype=jnp.int32)
        scales = jax.random.uniform(ks[2], (6, D, D // GROUP), dtype=jnp.float32)
        biases = jax.random.normal(ks[3], (6, D), dtype=jnp.float32) * 0.02
        lora_a = jax.random.normal(ks[4], (6, R, D), dtype=jnp.float32) * 0.02
        lora_b = jax.random.normal(ks[5], (6, D, R), dtype=jnp.float32) * 0.02
        ln_gamma = jnp.ones((3, D), dtype=jnp.float32)
        ln_beta = jnp.zeros((3, D), dtype=jnp.float32)
        return {'x': x, 'qweights': qweights, 'scales': scales, 'biases': biases, 'lora_a': lora_a, 'lora_b': lora_b, 'ln_gamma': ln_gamma, 'ln_beta': ln_beta}
    _L0_ffn_in = _L0_ffn_setup()
    _d = {'L0_attn_x': _L0_attn_in['x'], 'L0_attn_ln_w': _L0_attn_in['ln_w'], 'L0_attn_ln_b': _L0_attn_in['ln_b'], 'L0_attn_in_proj_w': _L0_attn_in['in_proj_w'], 'L0_attn_conv_w': _L0_attn_in['conv_w'], 'L0_attn_conv_b': _L0_attn_in['conv_b'], 'L0_attn_dt_bias': _L0_attn_in['dt_bias'], 'L0_attn_A_log': _L0_attn_in['A_log'], 'L0_attn_D': _L0_attn_in['D'], 'L0_attn_rms_w': _L0_attn_in['rms_w'], 'L0_attn_out_proj_w': _L0_attn_in['out_proj_w'], 'L0_ffn_qweights': _L0_ffn_in['qweights'], 'L0_ffn_scales': _L0_ffn_in['scales'], 'L0_ffn_biases': _L0_ffn_in['biases'], 'L0_ffn_lora_a': _L0_ffn_in['lora_a'], 'L0_ffn_lora_b': _L0_ffn_in['lora_b'], 'L0_ffn_ln_gamma': _L0_ffn_in['ln_gamma'], 'L0_ffn_ln_beta': _L0_ffn_in['ln_beta']}
    _x0 = _d['L0_attn_x']
    _d['L0_attn_x'] = jax.random.normal(jax.random.fold_in(jax.random.key(seed), 1), (8, 1024, 256), dtype=_x0.dtype)
    del _x0
    return _d

def reference(L0_attn_x, L0_attn_ln_w, L0_attn_ln_b, L0_attn_in_proj_w, L0_attn_conv_w, L0_attn_conv_b, L0_attn_dt_bias, L0_attn_A_log, L0_attn_D, L0_attn_rms_w, L0_attn_out_proj_w, L0_ffn_qweights, L0_ffn_scales, L0_ffn_biases, L0_ffn_lora_a, L0_ffn_lora_b, L0_ffn_ln_gamma, L0_ffn_ln_beta):

    def _L0_attn_ref(x, ln_w, ln_b, in_proj_w, conv_w, conv_b, dt_bias, A_log, D, rms_w, out_proj_w):
        import jax, jax.numpy as jnp
        import numpy as np
        D_MODEL = 256
        N_LAYERS = 2
        D_STATE = 64
        D_CONV = 4
        EXPAND = 2
        D_INNER = EXPAND * D_MODEL
        HEADDIM = D_STATE
        NHEADS = D_INNER // HEADDIM
        CONV_DIM = D_INNER + 2 * D_STATE
        D_IN_PROJ = 2 * D_INNER + 2 * D_STATE + NHEADS
        EPS = 1e-05

        def _layernorm(x, w, b):
            m = x.mean(-1, keepdims=True)
            v = ((x - m) ** 2).mean(-1, keepdims=True)
            return (x - m) * jax.lax.rsqrt(v + EPS) * w + b

        def _mamba2(u, in_w, conv_w, conv_b, dt_bias, A_log, Dp, rms_w, out_w):
            b, l, _ = u.shape
            zxbcdt = u @ in_w.T
            z, xBC, dt = jnp.split(zxbcdt, [D_INNER, D_INNER + CONV_DIM], axis=-1)
            dt = jax.nn.softplus(dt + dt_bias)
            xBC = jnp.transpose(xBC, (0, 2, 1))
            xBC = jax.lax.conv_general_dilated(xBC, conv_w[:, None, :], (1,), [(D_CONV - 1, 0)], dimension_numbers=('NCH', 'OIH', 'NCH'), feature_group_count=CONV_DIM)
            xBC = jnp.transpose(xBC, (0, 2, 1)) + conv_b
            xBC = jax.nn.silu(xBC)
            xh, Bm, Cm = jnp.split(xBC, [D_INNER, D_INNER + D_STATE], axis=-1)
            xh = xh.reshape(b, l, NHEADS, HEADDIM)
            A = -jnp.exp(A_log)
            dA = jnp.exp(dt * A)

            def step(state, inputs):
                dA_t, dt_t, x_t, B_t, C_t = inputs
                state = dA_t[:, :, None, None] * state + (dt_t[:, :, None] * x_t)[..., None] * B_t[:, None, None, :]
                y_t = jnp.einsum('bhpn,bn->bhp', state, C_t)
                return (state, y_t)
            xs = (jnp.moveaxis(dA, 1, 0), jnp.moveaxis(dt, 1, 0), jnp.moveaxis(xh, 1, 0), jnp.moveaxis(Bm, 1, 0), jnp.moveaxis(Cm, 1, 0))
            init = jnp.zeros((b, NHEADS, HEADDIM, D_STATE), u.dtype)
            _, ys = jax.lax.scan(step, init, xs)
            y = jnp.moveaxis(ys, 0, 1) + Dp[None, None, :, None] * xh
            y = y.reshape(b, l, D_INNER)
            y = y * jax.nn.silu(z)
            y = y * jax.lax.rsqrt(jnp.mean(y * y, -1, keepdims=True) + EPS) * rms_w
            return y @ out_w.T
        h = x
        for i in range(N_LAYERS):
            res = h
            h = _layernorm(h, ln_w[i], ln_b[i])
            h = _mamba2(h, in_proj_w[i], conv_w[i], conv_b[i], dt_bias[i], A_log[i], D[i], rms_w[i], out_proj_w[i])
            h = h + res
        return h

    def _L0_ffn_ref(x, qweights, scales, biases, lora_a, lora_b, ln_gamma, ln_beta):
        import jax, jax.numpy as jnp
        import numpy as np
        GROUP = 16
        EPS = 1e-05

        def _dequant(q, scale):
            w = q.astype(jnp.float32) / 7.5 - 1.0
            return w * jnp.repeat(scale, GROUP, axis=1)

        def _qlora_linear(x, q, scale, bias, la, lb):
            w = _dequant(q, scale)
            base = jnp.einsum('btd,od->bto', x, w) + bias
            lora = jnp.einsum('btr,or->bto', jnp.einsum('btd,rd->btr', x, la), lb)
            return base + lora

        def _layernorm(x, g, b):
            mu = jnp.mean(x, axis=-1, keepdims=True)
            var = jnp.mean(jnp.square(x - mu), axis=-1, keepdims=True)
            return (x - mu) * jax.lax.rsqrt(var + EPS) * g + b
        h = x
        for blk in range(3):
            i0, i1 = (2 * blk, 2 * blk + 1)
            y = _qlora_linear(h, qweights[i0], scales[i0], biases[i0], lora_a[i0], lora_b[i0])
            y = _layernorm(y, ln_gamma[blk], ln_beta[blk])
            y = jax.nn.gelu(y, approximate=False)
            y = _qlora_linear(y, qweights[i1], scales[i1], biases[i1], lora_a[i1], lora_b[i1])
            h = y + h
        return h
    x = L0_attn_x
    x = x + _L0_attn_ref(_layernorm(x, axis=-1), L0_attn_ln_w, L0_attn_ln_b, L0_attn_in_proj_w, L0_attn_conv_w, L0_attn_conv_b, L0_attn_dt_bias, L0_attn_A_log, L0_attn_D, L0_attn_rms_w, L0_attn_out_proj_w)
    x = x + _L0_ffn_ref(_layernorm(x, axis=-1), L0_ffn_qweights, L0_ffn_scales, L0_ffn_biases, L0_ffn_lora_a, L0_ffn_lora_b, L0_ffn_ln_gamma, L0_ffn_ln_beta)
    return x

_drawn_inputs = setup_inputs


def setup_inputs(seed=0):
    import zlib

    import numpy as np

    out = dict(_drawn_inputs(seed))
    spreads = {'L0_attn_ln_w': (1.0, 0.2),
     'L0_attn_ln_b': (0.0, 0.1),
     'L0_attn_conv_b': (0.0, 0.1),
     'L0_attn_D': (1.0, 0.2),
     'L0_attn_rms_w': (1.0, 0.2),
     'L0_ffn_ln_gamma': (1.0, 0.2),
     'L0_ffn_ln_beta': (0.0, 0.1)}
    factors = {'L0_ffn_biases': 8.0, 'L0_ffn_lora_a': 5.167, 'L0_ffn_lora_b': 5.056}
    for name, (base, spread) in spreads.items():
        noise = np.random.default_rng([zlib.crc32(name.encode()), seed]).standard_normal(out[name].shape)
        drawn = base * np.exp(spread * noise) if base else spread * noise
        out[name] = jnp.asarray(drawn.astype(out[name].dtype))
    for name, factor in factors.items():
        out[name] = (out[name] * factor).astype(out[name].dtype)
    return out
```

```python
from contextlib import ExitStack

import numpy as np

import concourse.bass as bass
from concourse import mybir

F32 = mybir.dt.float32
F32R = mybir.dt.float32r
BF16 = mybir.dt.bfloat16
I32 = mybir.dt.int32
ALU = mybir.AluOpType
ACT = mybir.ActivationFunctionType

P = 128
DM = 256
KD = DM // P
DI = 512
T = DI // P
NH = 8
HD = 64
NS = 64
TAPS = 4
NPROJ = 2 * DI + 2 * NS + NH
SEQ, LEN = 8, 1024
CHUNKS = LEN // P
NB = 4
GROUPS = SEQ // NB
ITEMS = CHUNKS * GROUPS
W = NB * P
HALO = TAPS - 1
EPS = 1e-5
QCONV = T + 1
PARTS = 3
ROWS = 64
BLOCKS = 3
RANK = 32
QGROUP = 16

C_IDENT, C_TRI, C_SUF, C_MASK, C_SEL, C_COL = 0, 128, 256, 384, 384 + NH * P, 384 + NH * P + 256
C_END = C_COL + 4


def constants():
    c = np.zeros((P, C_END), np.float32)
    i = np.arange(P)
    c[:, C_IDENT:C_IDENT + P] = np.eye(P)
    c[:, C_TRI:C_TRI + P] = i[:, None] <= i[None, :]
    c[:, C_SUF:C_SUF + P] = i[:, None] > i[None, :]
    for half in range(2):
        for dup in range(2):
            for part in range(PARTS):
                for h in range(NH):
                    row = ROWS * half + PARTS * NH * dup + NH * part + h
                    c[row, C_MASK + h * P:C_MASK + (h + 1) * P] = -1 if dup else 1
                    if not dup:
                        odd = h % 2
                        at = C_SEL + P * odd + HD * odd
                        c[row, at:at + HD] = 1
                    c[row, C_COL + 0] = dup
                    c[row, C_COL + 1] = 1 - dup
                    c[row, C_COL + 2] = 1 - dup
                    c[row, C_COL + 3] = dup
    return c


def wait(eng, sem, value):
    if isinstance(value, int) and value <= 0:
        return
    eng.wait_ge(sem, value)


def over_items(eng, step):
    step(0, 0, 0)
    step(1, 0, 1)
    with eng.Fori(0, CHUNKS - 2) as i:
        step(2 * i + 2, i + 1, 0)
        step(2 * i + 3, i + 1, 1)
    step(ITEMS - 2, CHUNKS - 1, 0)
    step(ITEMS - 1, CHUNKS - 1, 1)


def follows(n, by):
    return not isinstance(n, int) or n + by < ITEMS


MOMENTS = ("sum2", "gap", "within", "gap2", "spread", "mean")


def moments(nc, dve, tiles, stats, mom, var, s_stats, s_mom, s_var, n):
    at = {name: mom[:, i, :] for i, name in enumerate(MOMENTS)}
    for b in range(NB):
        nc.vector.bn_stats(stats[:, b, :], tiles[b]).then_inc(s_stats, 1)
    dve.wait_ge(s_stats, NB * n + NB)
    nc.vector.tensor_tensor(at["gap"], stats[:, :, 1], stats[:, :, 4], ALU.subtract).then_inc(s_mom, 1)
    nc.vector.tensor_tensor(at["within"], stats[:, :, 2], stats[:, :, 5], ALU.add).then_inc(s_mom, 1)
    nc.vector.tensor_tensor(at["sum2"], stats[:, :, 1], stats[:, :, 4], ALU.add).then_inc(s_mom, 1)
    dve.wait_ge(s_mom, 6 * n + 1)
    nc.vector.tensor_tensor(at["gap2"], at["gap"], at["gap"], ALU.mult).then_inc(s_mom, 1)
    dve.wait_ge(s_mom, 6 * n + 4)
    nc.vector.scalar_tensor_tensor(at["spread"], at["gap2"], DM / 4.0, at["within"], ALU.mult, ALU.add).then_inc(s_mom, 1)
    nc.vector.tensor_scalar(at["mean"], at["sum2"], 0.5, None, ALU.mult).then_inc(s_mom, 1)
    dve.wait_ge(s_mom, 6 * n + 5)
    nc.vector.tensor_scalar(var, at["spread"], 1.0 / DM, EPS, ALU.mult, ALU.add).then_inc(s_var, 1)


def item_tokens(dram, chunk, group):
    view = dram.rearrange("(g b) (c p) d -> c g p b d", b=NB, p=P)
    if isinstance(chunk, int):
        return view[chunk, group]
    return view[bass.ds(chunk, 1), group].rearrange("a p b d -> (a p) b d")


def mamba_layer(nc, layer, first, src, dst, w):
    with ExitStack() as keep:
        def sb(name, shape, dt=F32, ctx=keep):
            return ctx.enter_context(nc.sbuf_tensor(f"L{layer}_{name}", shape, dt))


        whi = sb("whi", [P, KD, NPROJ], F32R)
        wlo = sb("wlo", [P, KD, NPROJ], F32R)
        wo = sb("wo", [P, T, DM])
        ident = sb("ident", [P, P])
        identb = sb("identb", [P, P], BF16)
        tri = sb("tri", [P, P])
        suffix = sb("suffix", [P, P])
        ones = sb("ones", [P, P])
        mask = sb("mask", [P, NH, P], BF16)
        sel = sb("sel", [P, 2, P], BF16)
        col = sb("col", [P, 4])
        pbias = sb("pbias", [P, 2 * T + 1])
        convw = sb("convw", [P, QCONV, TAPS])
        convb = sb("convb", [P, QCONV])
        dcol = sb("dcol", [P, T])
        dtb = sb("dtb", [P, NH])
        aneg = sb("aneg", [P, NH])
        power = sb("power", [P, NB])

        prepare_layer(nc, layer, w, locals())
        layer_items(nc, layer, first, src, dst, locals())


def prepare_layer(nc, layer, w, k):
    whi, wlo, wo, ident, identb, tri, suffix, ones, mask, sel, col = (
        k[x] for x in ("whi", "wlo", "wo", "ident", "identb", "tri", "suffix", "ones", "mask", "sel", "col"))
    pbias, convw, convb, dcol, dtb, aneg, power = (
        k[x] for x in ("pbias", "convw", "convb", "dcol", "dtb", "aneg", "power"))
    with ExitStack() as ctx:
        def sb(name, shape, dt=F32):
            return ctx.enter_context(nc.sbuf_tensor(f"L{layer}_{name}", shape, dt))

        def sem(name):
            return nc.alloc_semaphore(name=f"L{layer}_{name}")

        raw = sb("raw", [P, KD, NPROJ])
        full = sb("full", [P, KD, NPROJ])
        rawo = sb("rawo", [P, T, DM])
        lnw = sb("lnw", [P, KD])
        lnb = sb("lnb", [P, KD])
        lnb_rows = sb("lnb_rows", [P, KD, P])
        rmsw = sb("rmsw", [P, T])
        dtbias = sb("dtbias", [P, NH])
        alog = sb("alog", [P, NH])
        aexp = sb("aexp", [P, NH])
        maskf = sb("maskf", [P, NH * P])
        self_ = sb("self", [P, 2 * P])
        acc = ctx.enter_context(nc.psum_tensor(f"L{layer}_pbias_ps", [P, 512], F32))
        accd = ctx.enter_context(nc.psum_tensor(f"L{layer}_pdt_ps", [P, 512], F32))
        weights_in, small_in = sem("weights_in"), sem("small_in")
        ones_ready, rows_ready, full_ready, hi_ready = sem("ones_ready"), sem("rows_ready"), sem("full_ready"), sem("hi_ready")
        bias_summed, aexp_ready, prepared = sem("bias_summed"), sem("aexp_ready"), sem("prepared")
        N_WEIGHTS, N_SMALL = 2, 15

        block = ctx.enter_context(nc.Block())

        @block.sync
        def _(sp):
            sp.dma_start(raw[:, :, :], w["in_proj"][layer].rearrange("(k p) n -> p k n", p=P)).then_inc(weights_in, 16)
            sp.dma_start(rawo[:, :, :], w["out_proj"][layer].rearrange("(t p) n -> p t n", p=P)).then_inc(weights_in, 16)
            small = [
                (lnw[:, :], w["ln_w"][layer]),
                (lnb[:, :], w["ln_b"][layer]),
                (rmsw[:, :], w["rms_w"][layer]),
                (convw[:, :, :], w["conv_w"][layer].rearrange("(q p) k -> p q k", p=P)),
                (convb[:, :], w["conv_b"][layer]),
                (dtbias[:, :], w["dt_bias"][layer].partition_broadcast(P)),
                (alog[:, :], w["A_log"][layer].partition_broadcast(P)),
                (ident[:, :], w["constants"][:, C_IDENT:C_IDENT + P]),
                (tri[:, :], w["constants"][:, C_TRI:C_TRI + P]),
                (suffix[:, :], w["constants"][:, C_SUF:C_SUF + P]),
                (maskf[:, :], w["constants"][:, C_MASK:C_MASK + NH * P]),
                (self_[:, :], w["constants"][:, C_SEL:C_SEL + 2 * P]),
                (col[:, :], w["constants"][:, C_COL:C_COL + 4]),
            ]
            for odd in range(2):
                heads = w["D"][layer, odd]
                small.append((dcol[HD * odd:HD * odd + HD, :], heads.partition_broadcast(HD)))
            assert len(small) == N_SMALL
            for to, of in small:
                sp.dma_start(to, of).then_inc(small_in, 16)

        @block.tensor
        def _(pe):
            pe.wait_ge(weights_in, 16 * N_WEIGHTS)
            pe.wait_ge(small_in, 16 * N_SMALL)
            for ct in range(2 * T + 1):
                for kd in range(KD):
                    nc.tensor.matmul(acc[:, ct:ct + 1], raw[:, kd, ct * P:(ct + 1) * P], lnb[:, kd:kd + 1],
                                     start=kd == 0, stop=kd == KD - 1)
            pe.wait_ge(rows_ready, KD)
            for kd in range(KD):
                last = nc.tensor.matmul(accd[:, 0:NH], lnb_rows[:, kd, :], raw[:, kd, NPROJ - NH:NPROJ],
                                        start=kd == 0, stop=kd == KD - 1)
            last.then_inc(bias_summed, 1)

        @block.scalar
        def _(act):
            act.wait_ge(small_in, 16 * N_SMALL)
            nc.scalar.activation(aexp[:, :], alog[:, :], ACT.Exp).then_inc(aexp_ready, 1)

        @block.vector
        def _(dve):
            nc.vector.memset(ones[:, :], 1.0).then_inc(ones_ready, 1)
            nc.vector.memset(power[:, :], -0.5)
            dve.wait_ge(ones_ready, 1)
            dve.wait_ge(small_in, 16 * N_SMALL)
            dve.wait_ge(weights_in, 16 * N_WEIGHTS)
            for kd in range(KD):
                nc.vector.tensor_scalar(lnb_rows[:, kd, :], ones[:, :], lnb[:, kd:kd + 1], None, ALU.mult).then_inc(rows_ready, 1)
            for kd in range(KD):
                nc.vector.tensor_scalar(full[:, kd, :], raw[:, kd, :], lnw[:, kd:kd + 1], None, ALU.mult).then_inc(full_ready, 1)
            dve.wait_ge(full_ready, KD)
            nc.vector.tensor_copy(whi[:, :, :], full[:, :, :]).then_inc(hi_ready, 1)
            dve.wait_ge(hi_ready, 1)
            nc.vector.tensor_tensor(wlo[:, :, :], full[:, :, :], whi[:, :, :].bitcast(F32), ALU.subtract)
            for t in range(T):
                nc.vector.tensor_scalar(wo[:, t, :], rawo[:, t, :], rmsw[:, t:t + 1], None, ALU.mult)
            nc.vector.tensor_copy(identb[:, :], ident[:, :])
            nc.vector.tensor_copy(mask[:, :, :], maskf[:, :].rearrange("p (h i) -> p h i", h=NH))
            nc.vector.tensor_copy(sel[:, :, :], self_[:, :].rearrange("p (o m) -> p o m", o=2))
            dve.wait_ge(aexp_ready, 1)
            nc.vector.tensor_scalar(aneg[:, :], aexp[:, :], -1.0, None, ALU.mult)
            dve.wait_ge(bias_summed, 1)
            nc.vector.tensor_copy(pbias[:, :], acc[:, 0:2 * T + 1])
            nc.vector.tensor_tensor(dtb[:, :], accd[:, 0:NH], dtbias[:, :], ALU.add).then_inc(prepared, 1)
            dve.wait_ge(prepared, 1)


def layer_items(nc, layer, first, src, dst, k):
    whi, wlo, wo, ident, identb, tri, suffix, ones, mask, sel, col = (
        k[x] for x in ("whi", "wlo", "wo", "ident", "identb", "tri", "suffix", "ones", "mask", "sel", "col"))
    pbias, convw, convb, dcol, dtb, aneg, power = (
        k[x] for x in ("pbias", "convw", "convb", "dcol", "dtb", "aneg", "power"))
    with ExitStack() as ctx:
        def sb(name, shape, dt=F32):
            return ctx.enter_context(nc.sbuf_tensor(f"L{layer}_{name}", shape, dt))

        def bank(name):
            return ctx.enter_context(nc.psum_tensor(f"L{layer}_{name}", [P, 512], F32))

        def sem(name):
            return nc.alloc_semaphore(name=f"L{layer}_{name}")

        hin = [sb(f"hin{p}", [P, NB, DM]) for p in range(2)]
        hres = [sb(f"hres{p}", [P, NB, DM]) for p in range(2)]
        hout = sb("hout", [P, NB, DM])
        stats0, mom0, var0, rstd0 = sb("stats0", [P, NB, 6]), sb("mom0", [P, 6, NB]), sb("var0", [P, NB]), sb("rstd0", [P, NB])
        stats, mom, var, rstd = sb("stats", [P, NB, 6]), sb("mom", [P, 6, NB]), sb("var", [P, NB]), sb("rstd", [P, NB])
        normed = sb("normed", [P, NB, DM])
        uhi, ulo = sb("uhi", [P, KD, W], F32R), sb("ulo", [P, KD, W], F32R)
        xpad = sb("xpad", [P, QCONV, NB, HALO + P])
        halo = [sb(f"halo{g}", [P, QCONV, NB, HALO]) for g in range(GROUPS)]
        xc = [sb(f"xc{p}", [P, QCONV, W]) for p in range(2)]
        cc = sb("cc", [P, W])
        sz = sb("sz", [P, T, W])
        dtraw, dtabs, dtexp, dtln = (sb(x, [P, NB, NH]) for x in ("dtraw", "dtabs", "dtexp", "dtln"))
        dtv = [sb(f"dtv{p}", [P, NB, NH]) for p in range(2)]
        da = sb("da", [P, NB, NH])
        sums = sb("sums", [P, 3, NB, NH])
        decay = [sb(f"decay{p}", [P, 2, NB, NH]) for p in range(2)]
        rest1, rest2 = sb("rest1", [P, NB, NH]), sb("rest2", [P, NB, NH])
        cum3 = sb("cum3", [P, NB, ROWS], BF16)
        dstat, dmovT = sb("dstat", [P, 2, P], BF16), sb("dmovT", [P, 2, P], BF16)
        dmov = sb("dmov", [P, 2, NH, P], BF16)
        expd = sb("expd", [P, 2, NH // 2, P])
        gm = sb("gm", [P, NB, P])
        m = sb("m", [P, NB, NH, P])
        dtx = sb("dtx", [P, NB, NH, HD])
        wx = sb("wx", [P, NB, NH, HD])
        bt = sb("bt", [P, NB, NS])
        ecum = sb("ecum", [P, 2, T, P])
        cs = sb("cs", [P, NB, T, P])
        state = [sb(f"state{g}", [P, NB, T, P]) for g in range(GROUPS)]
        sdec = sb("sdec", [P, NB, NH, HD])
        yg = sb("yg", [P, T, W])
        sq = sb("sq", [P, T, W])
        ssq, rrms = sb("ssq", [P, NB]), sb("rrms", [P, NB])
        front = [bank(f"front{i}") for i in range(2)]
        dbank = [bank(f"dbank{i}") for i in range(2)]
        ybank = [bank(f"ybank{i}") for i in range(2)]
        mix = [bank(f"mix{i}") for i in range(2)]

        h_in = [sem(f"h_in{p}") for p in range(2)]
        res_in = [sem(f"res_in{p}") for p in range(2)]
        cc_in = sem("cc_in")
        stored = sem("stored")
        cleared = sem("cleared")
        ln0_stats, ln0_mom, ln0_var, ln0_rstd, ln0_done = (sem(x) for x in ("ln0_stats", "ln0_mom", "ln0_var", "ln0_rstd", "ln0_done"))
        ln_stats, ln_mom, ln_var, ln_rstd, ln_done = (sem(x) for x in ("ln_stats", "ln_mom", "ln_var", "ln_rstd", "ln_done"))
        u_turned, u_hi, u_lo = sem("u_turned"), sem("u_hi"), sem("u_lo")
        proj = sem("proj")
        dt_biased, dt_abs, dt_exp, dt_ln, dt_done, da_done = (sem(x) for x in ("dt_biased", "dt_abs", "dt_exp", "dt_ln", "dt_done", "da_done"))
        da_summed, sums_out, decay_done = sem("da_summed"), sem("sums_out"), sem("decay_done")
        split = sem("split")
        cum_turned, dops, dmov_done = sem("cum_turned"), sem("dops"), sem("dmov_done")
        halo_set, halo_kept = sem("halo_set"), sem("halo_kept")
        x_raw, tap0, taps, conved = sem("x_raw"), sem("tap0"), sem("taps"), sem("conved")
        z_done = sem("z_done")
        g_done, gm_done = sem("g_done"), sem("gm_done")
        d_ready, d_abs, d_exp, m_done = sem("d_ready"), sem("d_abs"), sem("d_exp"), sem("m_done")
        xt_done, dtx_done, wx_done = sem("xt_done"), sem("dtx_done"), sem("wx_done")
        bt_turned, bt_done = sem("bt_turned"), sem("bt_done")
        ec_ready, ec_exp, cs_done = sem("ec_ready"), sem("ec_exp"), sem("cs_done")
        st_ready, sdec_done, state_done = sem("st_ready"), sem("sdec_done"), sem("state_done")
        y_ready, y_skip, y_gated, y_sq = sem("y_ready"), sem("y_skip"), sem("y_gated"), sem("y_sq")
        ss_ready, ss_done, rr_done = sem("ss_ready"), sem("ss_done"), sem("rr_done")
        o_ready, h_done = sem("o_ready"), sem("h_done")

        QORDER = [T, 0, 1, 2, 3]
        N_PROJ = 1 + QCONV + T

        block = ctx.enter_context(nc.Block())

        @block.sync
        def _(sp):
            def load_in(n, c, p):
                wait(sp, ln0_done if first else ln_done, n - 1)
                sp.dma_start(hin[p][:, :, :], item_tokens(src, c, p)).then_inc(h_in[p], 16)

            def load_res(n, c, p):
                wait(sp, h_done, NB * (n - 1))
                sp.dma_start(hres[p][:, :, :], item_tokens(src, c, p)).then_inc(res_in[p], 16)

            def store(n, c, p):
                sp.wait_ge(h_done, NB * (n + 1))
                sp.dma_start(item_tokens(dst, c, p), hout[:, :, :]).then_inc(stored, 16)

            for p in range(2):
                load_in(p, 0, p)
                if not first:
                    load_res(p, 0, p)

            def step(n, c, p):
                if follows(n, 2):
                    load_in(n + 2, c + 1, p)
                store(n, c, p)
                if not first and follows(n, 2):
                    load_res(n + 2, c + 1, p)

            over_items(sp, step)
            sp.wait_ge(stored, 16 * ITEMS)

        @block.tensor
        def _(pe):
            def turn_u(n):
                pe.wait_ge(ln_done, n + 1)
                wait(pe, z_done, T * n)
                for kd in range(KD):
                    for b in range(NB):
                        last = nc.tensor.transpose(front[kd][:, b * P:(b + 1) * P], normed[:, b, kd * P:(kd + 1) * P], ident[:, :])
                    last.then_inc(u_turned, 1)

            def project_dt(n):
                pe.wait_ge(u_lo, KD * n + KD)
                for b in range(NB):
                    passes = [(kd, a, ww) for kd in range(KD) for a, ww in ((uhi, whi), (uhi, wlo), (ulo, whi))]
                    for i, (kd, a, ww) in enumerate(passes):
                        last = nc.tensor.matmul(front[0][:, b * NH:(b + 1) * NH], a[:, kd, b * P:(b + 1) * P],
                                                ww[:, kd, NPROJ - NH:NPROJ], start=i == 0, stop=i == len(passes) - 1)
                last.then_inc(proj, 1)

            def project(to, tile):
                passes = [(kd, a, ww) for kd in range(KD) for ww, a in ((whi, uhi), (whi, ulo), (wlo, uhi))]
                for i, (kd, a, ww) in enumerate(passes):
                    last = nc.tensor.matmul(to[:, :], ww[:, kd, tile * P:(tile + 1) * P], a[:, kd, :],
                                            start=i == 0, stop=i == len(passes) - 1)
                last.then_inc(proj, 1)

            def project_conv(n, i):
                if i == 0:
                    pe.wait_ge(u_lo, KD * n + KD)
                elif i == 1:
                    pe.wait_ge(dt_biased, n + 1)
                else:
                    pe.wait_ge(x_raw, QCONV * n + i - 1)
                project(front[(i + 1) % 2], T + QORDER[i])

            def sum_da(n):
                pe.wait_ge(da_done, n + 1)
                pe.wait_ge(x_raw, QCONV * n + 4)
                for i, matrix in enumerate((tri, suffix, ones)):
                    last = nc.tensor.matmul(front[0][:, i * NB * NH:(i + 1) * NB * NH], matrix[:, :],
                                            da[:, :, :].rearrange("p b h -> p (b h)"), start=True, stop=True)
                last.then_inc(da_summed, 1)

            def turn_cum(n):
                pe.wait_ge(x_raw, QCONV * n + 5)
                pe.wait_ge(split, 5 * n + 5)
                for pair in range(2):
                    last = nc.tensor.transpose(front[1][:, pair * P // 2:(pair + 1) * P // 2].bitcast(BF16),
                                               cum3[:, 2 * pair:2 * pair + 2, :].rearrange("p b r -> p (b r)"), identb[:, :])
                last.then_inc(cum_turned, 1)

            def project_z(n, t):
                if t == 0:
                    pe.wait_ge(sums_out, n + 1)
                elif t == 1:
                    pe.wait_ge(dops, 2 * n + 2)
                else:
                    pe.wait_ge(z_done, T * n + t - 1)
                project(front[t % 2], t)

            def scores(n, p):
                pe.wait_ge(cc_in, 32 * (n + 1))
                wait(pe, h_done, NB * n)
                for b in range(NB):
                    last = nc.tensor.matmul(mix[0][:, b * P:(b + 1) * P], xc[p][0:NS, T, b * P:(b + 1) * P],
                                            cc[0:NS, b * P:(b + 1) * P], start=True, stop=True)
                last.then_inc(g_done, 1)

            def decays(n, q):
                b, half = q // 2, q % 2
                if q == 0:
                    pe.wait_ge(dmov_done, 2 * n + 2)
                wait(pe, d_abs, 8 * n + q - 1)
                rows = slice(ROWS * (b % 2), ROWS * (b % 2) + ROWS)
                nc.tensor.matmul(dbank[half][:, :], dstat[rows, b // 2, :],
                                 dmov[rows, b // 2, 4 * half:4 * half + 4, :], start=True, stop=True).then_inc(d_ready, 1)

            def turn_x(n, p, b):
                if b == 0:
                    pe.wait_ge(conved, QCONV * n + QCONV)
                    wait(pe, h_done, NB * n)
                elif b == 1:
                    pe.wait_ge(gm_done, n + 1)
                else:
                    pe.wait_ge(dtx_done, NB * n + b - 1)
                for t in range(T):
                    last = nc.tensor.transpose(mix[(b + 1) % 2][:, t * P:(t + 1) * P], xc[p][:, t, b * P:(b + 1) * P], ident[:, :])
                last.then_inc(xt_done, 1)

            def turn_b(n, p):
                pe.wait_ge(dtx_done, NB * n + 3)
                for b in range(NB):
                    last = nc.tensor.transpose(mix[1][:, b * P:(b + 1) * P], xc[p][:, T, b * P:(b + 1) * P], ident[:, :])
                last.then_inc(bt_turned, 1)

            def carry(n, b):
                if b == 0:
                    pe.wait_ge(dtx_done, NB * n + 4)
                elif b == 1:
                    pe.wait_ge(bt_done, n + 1)
                else:
                    pe.wait_ge(ec_exp, NB * n + b - 1)
                rows = slice(ROWS * (b % 2), ROWS * (b % 2) + ROWS)
                moving = dmov[rows, b // 2, :, :].rearrange("r (t o) i -> r t o i", o=2)
                for odd in range(2):
                    last = nc.tensor.matmul(mix[b % 2][:, :], sel[rows, odd, :], moving[:, :, odd, :], start=odd == 0, stop=odd == 1)
                last.then_inc(ec_ready, 1)

            def new_state(n, s):
                pe.wait_ge(ec_exp, NB * n + 3 + s)
                pe.wait_ge(wx_done, NB * n + 2 * s + 2)
                pe.wait_ge(bt_done, n + 1)
                for b in (2 * s, 2 * s + 1):
                    values = wx[:, b, :, :].rearrange("p (t o) d -> p t o d", o=2)
                    for odd in range(2):
                        last = nc.tensor.matmul(mix[s][HD * odd:HD * odd + HD, (b % 2) * T * HD:(b % 2 + 1) * T * HD],
                                                bt[:, b, :], values[:, :, odd, :], start=True, stop=True)
                last.then_inc(st_ready, 1)

            def outputs(n, p, t):
                if t == 0:
                    pe.wait_ge(m_done, 8 * n + 8)
                    pe.wait_ge(cs_done, NB * n + NB)
                    wait(pe, state_done, 4 * (n - 1))
                    if isinstance(n, int) and n < GROUPS:
                        pe.wait_ge(cleared, 1)
                wait(pe, y_skip, T * n + t - 1)
                to = ybank[t % 2]
                for b in range(NB):
                    at = slice(b * P, (b + 1) * P)
                    nc.tensor.matmul(to[:, at], state[p][:, b, t, :], cs[:, b, t, :], start=True, stop=False, skip_group_check=True)
                    for odd in range(2):
                        last = nc.tensor.matmul(to[HD * odd:HD * odd + HD, at], dtx[:, b, 2 * t + odd, :], m[:, b, 2 * t + odd, :],
                                                start=False, stop=True, skip_group_check=True)
                last.then_inc(y_ready, 1)

            def square_sums(n):
                pe.wait_ge(y_sq, T * n + T)
                pe.wait_ge(state_done, 4 * n + 2)
                for b in range(NB):
                    for t in range(T):
                        last = nc.tensor.matmul(mix[0][:, b:b + 1], sq[:, t, b * P:(b + 1) * P], ones[:, 0:1],
                                                start=t == 0, stop=t == T - 1)
                last.then_inc(ss_ready, 1)

            def result(n, s):
                if s == 0:
                    pe.wait_ge(state_done, 4 * n + 4)
                else:
                    pe.wait_ge(ss_done, n + 1)
                for b in (2 * s, 2 * s + 1):
                    for t in range(T):
                        last = nc.tensor.matmul(mix[1 - s][:, (b % 2) * DM:(b % 2 + 1) * DM], yg[:, t, b * P:(b + 1) * P],
                                                wo[:, t, :], start=t == 0, stop=t == T - 1)
                last.then_inc(o_ready, 1)

            def front_part(n):
                turn_u(n)
                project_dt(n)
                for i in range(QCONV):
                    project_conv(n, i)
                sum_da(n)
                turn_cum(n)
                for t in range(T):
                    project_z(n, t)

            def step(n, c, p):
                more = follows(n, 1)
                if more:
                    turn_u(n + 1)
                scores(n, p)
                decays(n, 0)
                decays(n, 1)
                turn_x(n, p, 0)
                decays(n, 2)
                turn_x(n, p, 1)
                decays(n, 3)
                turn_x(n, p, 2)
                decays(n, 4)
                turn_x(n, p, 3)
                decays(n, 5)
                turn_b(n, p)
                decays(n, 6)
                decays(n, 7)
                if more:
                    project_dt(n + 1)
                    project_conv(n + 1, 0)
                    project_conv(n + 1, 1)
                for b in range(NB):
                    carry(n, b)
                if more:
                    for i in range(2, QCONV):
                        project_conv(n + 1, i)
                for s in range(2):
                    new_state(n, s)
                for t in range(T):
                    outputs(n, p, t)
                if more:
                    sum_da(n + 1)
                    turn_cum(n + 1)
                    for t in range(T):
                        project_z(n + 1, t)
                square_sums(n)
                for s in range(2):
                    result(n, s)

            front_part(0)
            over_items(pe, step)

        @block.scalar
        def _(act):
            def round_u(n):
                for kd in range(KD):
                    act.wait_ge(u_turned, KD * n + kd + 1)
                    if kd == 0:
                        wait(act, proj, N_PROJ * n)
                    nc.scalar.activation(uhi[:, kd, :], front[kd][:, :], ACT.Copy).then_inc(u_hi, 1)

            def softplus(n):
                act.wait_ge(dt_biased, n + 1)
                nc.scalar.activation(dtabs[:, :, :], dtraw[:, :, :], ACT.Abs).then_inc(dt_abs, 1)
                act.wait_ge(dt_abs, n + 1)
                nc.scalar.activation(dtexp[:, :, :], dtabs[:, :, :], ACT.Exp, scale=-1.0).then_inc(dt_exp, 1)
                act.wait_ge(dt_exp, n + 1)
                nc.scalar.activation(dtln[:, :, :], dtexp[:, :, :], ACT.Ln, bias=1.0).then_inc(dt_ln, 1)

            def raw_conv(n, p, i):
                q = QORDER[i]
                act.wait_ge(proj, N_PROJ * n + 2 + i)
                wait(act, taps, 3 * QCONV * n)
                if i == 0:
                    wait(act, halo_kept, n)
                nc.scalar.activation(xpad[:, q, :, HALO:], front[(i + 1) % 2][:, :].rearrange("p (b i) -> p b i", b=NB),
                                     ACT.Identity, bias=pbias[:, T + q:T + q + 1]).then_inc(x_raw, 1)
                act.wait_ge(x_raw, QCONV * n + i + 1)
                if i == 0:
                    act.wait_ge(halo_set, n + 1)
                    wait(act, h_done, NB * (n - 1))
                nc.scalar.activation(xc[p][:, q, :].rearrange("p (b i) -> p b i", b=NB), xpad[:, q, :, 0:P],
                                     ACT.Copy, scale=convw[:, q, 0:1]).then_inc(tap0, 1)

            def silu_conv(n, p):
                for i, q in enumerate(QORDER):
                    act.wait_ge(taps, 3 * QCONV * n + 3 * i + 3)
                    nc.scalar.activation(xc[p][:, q, :], xc[p][:, q, :], ACT.Silu, bias=convb[:, q:q + 1]).then_inc(conved, 1)

            def double_c(n, p):
                act.wait_ge(conved, QCONV * n + 1)
                wait(act, cs_done, NB * n)
                wait(act, g_done, n)
                for half in range(2):
                    act.dma_start(cc[half * NS:(half + 1) * NS, :], xc[p][NS:2 * NS, T, :]).then_inc(cc_in, 16)

            def exp_sums(n, p):
                act.wait_ge(sums_out, n + 1)
                nc.scalar.activation(decay[p][:, :, :, :], sums[:, 1:3, :, :], ACT.Exp).then_inc(decay_done, 1)

            def silu_z(n, t):
                act.wait_ge(proj, N_PROJ * n + 2 + QCONV + t)
                nc.scalar.activation(sz[:, t, :], front[t % 2][:, :], ACT.Silu, bias=pbias[:, t:t + 1]).then_inc(z_done, 1)

            def exp_decay(n, q):
                act.wait_ge(d_ready, 8 * n + q + 1)
                wait(act, m_done, 8 * n + q - 1)
                nc.scalar.activation(expd[:, q % 2, :, :], dbank[q % 2][:, :].rearrange("p (h i) -> p h i", i=P), ACT.Abs).then_inc(d_abs, 1)
                act.wait_ge(d_abs, 8 * n + q + 1)
                nc.scalar.activation(expd[:, q % 2, :, :], expd[:, q % 2, :, :], ACT.Exp, scale=-1.0).then_inc(d_exp, 1)

            def keep_b(n):
                act.wait_ge(bt_turned, n + 1)
                wait(act, st_ready, 2 * n)
                nc.scalar.activation(bt[:, :, :], mix[1][:, :].rearrange("p (b c) -> p b c", b=NB)[:, :, 0:NS], ACT.Copy).then_inc(bt_done, 1)

            def exp_carry(n, b):
                act.wait_ge(ec_ready, NB * n + b + 1)
                wait(act, cs_done, NB * n + b - 1)
                nc.scalar.activation(ecum[:, b % 2, :, :], mix[b % 2][:, :].rearrange("p (t i) -> p t i", t=T),
                                     ACT.Exp).then_inc(ec_exp, 1)

            def square(n, t):
                act.wait_ge(y_gated, T * n + t + 1)
                nc.scalar.activation(sq[:, t, :], yg[:, t, :], ACT.Square).then_inc(y_sq, 1)

            def front_part(n, p):
                round_u(n)
                softplus(n)
                for i in range(QCONV):
                    raw_conv(n, p, i)
                exp_sums(n, p)
                silu_conv(n, p)
                double_c(n, p)
                for t in range(T):
                    silu_z(n, t)

            def step(n, c, p):
                more = follows(n, 1)
                if more:
                    round_u(n + 1)
                for q in range(6):
                    exp_decay(n, q)
                keep_b(n)
                for q in range(6, 8):
                    exp_decay(n, q)
                if more:
                    softplus(n + 1)
                    raw_conv(n + 1, 1 - p, 0)
                    raw_conv(n + 1, 1 - p, 1)
                for b in range(NB):
                    exp_carry(n, b)
                if more:
                    for i in range(2, QCONV):
                        raw_conv(n + 1, 1 - p, i)
                    exp_sums(n + 1, 1 - p)
                    silu_conv(n + 1, 1 - p)
                    double_c(n + 1, 1 - p)
                for t in range(T):
                    square(n, t)
                if more:
                    for t in range(T):
                        silu_z(n + 1, t)

            front_part(0, 0)
            over_items(act, step)

        @block.gpsimd
        def _(pool):
            def rsqrt(out, in_, ready, n, done):
                pool.wait_ge(ready, n + 1)
                nc.gpsimd.tensor_tensor(out[:, :], in_[:, :], power[:, :], ALU.pow).then_inc(done, 1)

            def norm(n):
                if first:
                    rsqrt(rstd0, var0, ln0_var, n, ln0_rstd)
                rsqrt(rstd, var, ln_var, n, ln_rstd)

            def to_end(n, p, b):
                pool.wait_ge(dtx_done, NB * n + b + 1)
                if b == 0:
                    pool.wait_ge(decay_done, n + 1)
                    wait(pool, st_ready, 2 * n)
                nc.gpsimd.tensor_tensor(wx[:, b, :, :], dtx[:, b, :, :], decay[p][:, 0, b, :].unsqueeze(2).broadcast_to([P, NH, HD]),
                                        ALU.mult).then_inc(wx_done, 1)

            def decay_state(n, p):
                wait(pool, state_done, 4 * n)
                if isinstance(n, int) and n < GROUPS:
                    pool.wait_ge(cleared, 1)
                nc.gpsimd.tensor_tensor(sdec[:, :, :, :], state[p][:, :, :, :].rearrange("p b t (o d) -> p b (t o) d", o=2),
                                        decay[p][:, 1, :, :].unsqueeze(3).broadcast_to([P, NB, NH, HD]), ALU.mult).then_inc(sdec_done, 1)

            def step(n, c, p):
                for b in range(NB):
                    to_end(n, p, b)
                decay_state(n, p)
                rsqrt(rrms, ssq, ss_done, n, rr_done)
                if follows(n, 2):
                    norm(n + 2)

            norm(0)
            norm(1)
            over_items(pool, step)

        @block.vector
        def _(dve):
            def layernorm(n, x, out, stats, mom, var, rstd, s_stats, s_mom, s_var, s_rstd, s_done, free):
                wait(dve, s_rstd, n)
                moments(nc, dve, [x[:, b, :] for b in range(NB)], stats, mom, var[:, :], s_stats, s_mom, s_var, n)
                dve.wait_ge(s_mom, 6 * n + 6)
                dve.wait_ge(s_rstd, n + 1)
                free()
                for b in range(NB):
                    last = nc.vector.tensor_scalar(out[:, b, :], x[:, b, :], mom[:, 5, b:b + 1], rstd[:, b:b + 1], ALU.subtract, ALU.mult)
                last.then_inc(s_done, 1)

            def norms(n, c, p):
                dve.wait_ge(h_in[p], 16 * (c + 1))
                source = hin[p]
                if first:
                    layernorm(n, hin[p], hres[p], stats0, mom0, var0, rstd0, ln0_stats, ln0_mom, ln0_var, ln0_rstd, ln0_done, lambda: None)
                    dve.wait_ge(ln0_done, n + 1)
                    source = hres[p]
                layernorm(n, source, normed, stats, mom, var, rstd, ln_stats, ln_mom, ln_var, ln_rstd, ln_done,
                          lambda: wait(dve, u_turned, KD * n))

            def rest_u(n):
                for kd in range(KD):
                    dve.wait_ge(u_hi, KD * n + kd + 1)
                    nc.vector.tensor_tensor(ulo[:, kd, :], front[kd][:, :], uhi[:, kd, :].bitcast(F32), ALU.subtract).then_inc(u_lo, 1)

            def bias_dt(n):
                dve.wait_ge(proj, N_PROJ * n + 1)
                nc.vector.tensor_tensor(dtraw[:, :, :], front[0][:, 0:NB * NH].rearrange("p (b h) -> p b h", b=NB),
                                        dtb[:, :].unsqueeze(1).broadcast_to([P, NB, NH]), ALU.add).then_inc(dt_biased, 1)

            def finish_dt(n, p):
                dve.wait_ge(dt_ln, n + 1)
                nc.vector.scalar_tensor_tensor(dtv[p][:, :, :], dtraw[:, :, :], 0.0, dtln[:, :, :], ALU.max, ALU.add).then_inc(dt_done, 1)
                dve.wait_ge(dt_done, n + 1)
                nc.vector.tensor_tensor(da[:, :, :], dtv[p][:, :, :], aneg[:, :].unsqueeze(1).broadcast_to([P, NB, NH]),
                                        ALU.mult).then_inc(da_done, 1)

            def split_sums(n):
                dve.wait_ge(da_summed, n + 1)
                wait(dve, decay_done, n)
                nc.vector.tensor_copy(sums[:, :, :, :].rearrange("p s b h -> p (s b h)"), front[0][:, 0:3 * NB * NH]).then_inc(sums_out, 1)
                wait(dve, cum_turned, n)

                def part(i, of):
                    to = cum3[:, :, 0:2 * PARTS * NH].rearrange("p b (d i h) -> p b d i h", d=2, i=PARTS)[:, :, :, i, :]
                    return nc.vector.tensor_copy(to, of.unsqueeze(2).broadcast_to([P, NB, 2, NH])).then_inc(split, 1)

                def rest(out, of, i):
                    return nc.vector.tensor_tensor(out[:, :, :], of, cum3[:, :, i * NH:(i + 1) * NH], ALU.subtract).then_inc(split, 1)

                cum = sums[:, 0, :, :]
                dve.wait_ge(sums_out, n + 1)
                part(0, cum)
                dve.wait_ge(split, 5 * n + 1)
                rest(rest1, cum, 0)
                dve.wait_ge(split, 5 * n + 2)
                part(1, rest1[:, :, :])
                dve.wait_ge(split, 5 * n + 3)
                rest(rest2, rest1[:, :, :], 1)
                dve.wait_ge(split, 5 * n + 4)
                part(2, rest2[:, :, :])

            def decay_operands(n):
                dve.wait_ge(cum_turned, n + 1)
                turned = front[1][:, 0:P].bitcast(BF16)
                for i, to in enumerate((dstat, dmovT)):
                    nc.vector.tensor_scalar(to[:, :, :].rearrange("p a j -> p (a j)"), turned, col[:, 2 * i:2 * i + 1], col[:, 2 * i + 1:2 * i + 2],
                                            ALU.mult, ALU.add).then_inc(dops, 1)
                dve.wait_ge(dops, 2 * n + 2)
                wait(dve, ec_ready, NB * n)
                for pair in range(2):
                    nc.vector.tensor_tensor(dmov[:, pair, :, :], dmovT[:, pair, :].unsqueeze(1).broadcast_to([P, NH, P]), mask[:, :, :],
                                            ALU.mult).then_inc(dmov_done, 1)

            def set_halo(n, g):
                wait(dve, taps, 3 * QCONV * n)
                wait(dve, halo_kept, n)
                if isinstance(n, int) and n < 2:
                    dve.wait_ge(cleared, 1)
                nc.vector.tensor_copy(xpad[:, :, :, 0:HALO].rearrange("p q b i -> p (q b) i"),
                                      halo[g][:, :, :, :].rearrange("p q b i -> p (q b) i")).then_inc(halo_set, 1)

            def keep_halo(n, g):
                dve.wait_ge(x_raw, QCONV * n + QCONV)
                nc.vector.tensor_copy(halo[g][:, :, :, :].rearrange("p q b i -> p (q b) i"),
                                      xpad[:, :, :, P:P + HALO].rearrange("p q b i -> p (q b) i")).then_inc(halo_kept, 1)

            def convolve(n, p, i):
                q = QORDER[i]
                to = xc[p][:, q, :].rearrange("p (b i) -> p b i", b=NB)
                dve.wait_ge(tap0, QCONV * n + i + 1)
                for tap in range(1, TAPS):
                    if tap > 1:
                        dve.wait_ge(taps, 3 * QCONV * n + 3 * i + tap - 1)
                    nc.vector.scalar_tensor_tensor(to, xpad[:, q, :, tap:tap + P], convw[:, q, tap:tap + 1], to, ALU.mult, ALU.add).then_inc(taps, 1)

            def mask_scores(n):
                dve.wait_ge(g_done, n + 1)
                nc.vector.tensor_tensor(gm[:, :, :], mix[0][:, :].rearrange("p (b i) -> p b i", b=NB),
                                        tri[:, :].unsqueeze(1).broadcast_to([P, NB, P]), ALU.mult).then_inc(gm_done, 1)

            def weigh(n, q):
                b, half = q // 2, q % 2
                dve.wait_ge(d_exp, 8 * n + q + 1)
                if q == 0:
                    dve.wait_ge(gm_done, n + 1)
                nc.vector.tensor_tensor(m[:, b, 4 * half:4 * half + 4, :], expd[:, half, :, :],
                                        gm[:, b, :].unsqueeze(1).broadcast_to([P, NH // 2, P]), ALU.mult).then_inc(m_done, 1)

            def scale_x(n, p, b):
                dve.wait_ge(xt_done, NB * n + b + 1)
                nc.vector.tensor_tensor(dtx[:, b, :, :], mix[(b + 1) % 2][:, :].rearrange("p (h d) -> p h d", h=NH),
                                        dtv[p][:, b, :].unsqueeze(2).broadcast_to([P, NH, HD]), ALU.mult).then_inc(dtx_done, 1)

            def scale_c(n, b):
                dve.wait_ge(ec_exp, NB * n + b + 1)
                nc.vector.tensor_tensor(cs[:, b, :, :], ecum[:, b % 2, :, :], cc[:, b * P:(b + 1) * P].unsqueeze(1).broadcast_to([P, T, P]),
                                        ALU.mult).then_inc(cs_done, 1)

            def skip(n, p, t):
                dve.wait_ge(y_ready, T * n + t + 1)
                nc.vector.scalar_tensor_tensor(yg[:, t, :], xc[p][:, t, :], dcol[:, t:t + 1], ybank[t % 2][:, :], ALU.mult, ALU.add).then_inc(y_skip, 1)

            def gate(n, t):
                dve.wait_ge(y_skip, T * n + t + 1)
                if t == 0:
                    dve.wait_ge(z_done, T * n + T)
                nc.vector.tensor_tensor(yg[:, t, :], yg[:, t, :], sz[:, t, :], ALU.mult).then_inc(y_gated, 1)

            def add_state(n, p):
                dve.wait_ge(sdec_done, n + 1)
                for s in range(2):
                    dve.wait_ge(st_ready, 2 * n + s + 1)
                    for odd in range(2):
                        half = slice(HD * odd, HD * odd + HD)
                        nc.vector.tensor_tensor(state[p][half, 2 * s:2 * s + 2, :, half], mix[s][half, :].rearrange("p (b t d) -> p b t d", b=2, t=T),
                                                sdec[half, 2 * s:2 * s + 2, :, :].rearrange("p b (t o) d -> p b t o d", o=2)[:, :, :, odd, :], ALU.add).then_inc(state_done, 1)

            def mean_square(n):
                dve.wait_ge(ss_ready, n + 1)
                nc.vector.tensor_scalar(ssq[:, :], mix[0][:, 0:NB], 1.0 / DI, EPS, ALU.mult, ALU.add).then_inc(ss_done, 1)

            def finish(n, c, p):
                dve.wait_ge(rr_done, n + 1)
                wait(dve, stored, 16 * n)
                if not first:
                    dve.wait_ge(res_in[p], 16 * (c + 1))
                for b in range(NB):
                    dve.wait_ge(o_ready, 2 * n + b // 2 + 1)
                    nc.vector.scalar_tensor_tensor(hout[:, b, :], mix[1 - b // 2][:, (b % 2) * DM:(b % 2 + 1) * DM], rrms[:, b:b + 1],
                                                   hres[p][:, b, :], ALU.mult, ALU.add).then_inc(h_done, 1)

            def front_part(n, p):
                rest_u(n)
                set_halo(n, p)
                bias_dt(n)
                finish_dt(n, p)
                for i in range(QCONV):
                    convolve(n, p, i)
                keep_halo(n, p)
                split_sums(n)
                decay_operands(n)

            def step(n, c, p):
                more = follows(n, 1)
                if more:
                    rest_u(n + 1)
                    set_halo(n + 1, 1 - p)
                mask_scores(n)
                weigh(n, 0)
                scale_x(n, p, 0)
                weigh(n, 1)
                scale_x(n, p, 1)
                weigh(n, 2)
                scale_x(n, p, 2)
                weigh(n, 3)
                scale_x(n, p, 3)
                for q in range(4, 8):
                    weigh(n, q)
                if more:
                    bias_dt(n + 1)
                    finish_dt(n + 1, 1 - p)
                    convolve(n + 1, 1 - p, 0)
                    convolve(n + 1, 1 - p, 1)
                for b in range(NB):
                    scale_c(n, b)
                if more:
                    for i in range(2, QCONV):
                        convolve(n + 1, 1 - p, i)
                    keep_halo(n + 1, 1 - p)
                for t in range(T):
                    skip(n, p, t)
                    gate(n, t)
                add_state(n, p)
                if more:
                    split_sums(n + 1)
                    decay_operands(n + 1)
                mean_square(n)
                finish(n, c, p)
                if follows(n, 2):
                    norms(n + 2, c + 1, p)

            for g in range(GROUPS):
                nc.vector.memset(halo[g][:, :, :, :], 0.0)
                nc.vector.memset(state[g][:, :, :, :], 0.0)
            nc.vector.memset(cum3[:, :, :], 0.0).then_inc(cleared, 1)
            dve.wait_ge(cleared, 1)
            norms(0, 0, 0)
            front_part(0, 0)
            norms(1, 0, 1)
            over_items(dve, step)


def mlp(nc, h, x, out, w):
    with ExitStack() as keep:
        def sb(name, shape, dt=F32):
            return keep.enter_context(nc.sbuf_tensor(f"M_{name}", shape, dt))

        whi = sb("whi", [P, 2 * BLOCKS, KD, DM], F32R)
        wlo = sb("wlo", [P, 2 * BLOCKS, KD, DM], F32R)
        ident = sb("ident", [P, P])
        rowsel = sb("rowsel", [PARTS * 32, P], BF16)
        bias3 = sb("bias3", [PARTS * 32, BLOCKS, DM], BF16)
        bias = sb("bias", [P, BLOCKS, KD])
        gamma = sb("gamma", [P, BLOCKS, KD])
        beta = sb("beta", [P, BLOCKS, KD])
        power = sb("power", [P, NB])
        prepare_mlp(nc, w, locals())
        mlp_items(nc, h, x, out, locals())


def prepare_mlp(nc, w, k):
    whi, wlo, ident, rowsel, bias3, bias, gamma, beta, power = (
        k[n] for n in ("whi", "wlo", "ident", "rowsel", "bias3", "bias", "gamma", "beta", "power"))
    N = 2 * BLOCKS
    with ExitStack() as ctx:
        def sb(name, shape, dt=F32):
            return ctx.enter_context(nc.sbuf_tensor(f"M_{name}", shape, dt))

        def sem(name):
            return nc.alloc_semaphore(name=f"M_{name}")

        q = sb("q", [P, N, KD, DM], I32)
        steps = sb("steps", [P, N, KD, DM])
        scaled = sb("scaled", [P, 2, KD, DM])
        full = sb("full", [P, N, KD, DM])
        scales = sb("scales", [DM // QGROUP, N, DM])
        spread = sb("spread", [DM // QGROUP, DM])
        la = sb("la", [RANK, N, DM])
        lb = sb("lb", [RANK, N, DM])
        brow = sb("brow", [P, BLOCKS, DM])
        part = [sb(f"part{i}", [P, BLOCKS, DM], BF16) for i in range(PARTS)]
        rest = [sb(f"rest{i}", [P, BLOCKS, DM]) for i in range(PARTS - 1)]
        rowself = sb("rowself", [PARTS * 32, P])
        scale_ps = [ctx.enter_context(nc.psum_tensor(f"M_scale_ps{i}", [P, KD, DM], F32)) for i in range(2)]
        lora_ps = [ctx.enter_context(nc.psum_tensor(f"M_lora_ps{i}", [P, KD, DM], F32)) for i in range(2)]
        loaded, spreadout, stepped, scaled_done, full_done, hi_done = (
            sem(x) for x in ("loaded", "spreadout", "stepped", "scaled_done", "full_done", "hi_done"))
        split, prepared = sem("split"), sem("prepared")
        block = ctx.enter_context(nc.Block())
        N_LOADS = 14

        @block.sync
        def _(sp):
            loads = [
                (q[:, :, :, :], w["qweights"].rearrange("j (k p) o -> p j k o", p=P)),
                (scales[:, :, :], w["scales"].rearrange("j g o -> g j o")),
                (spread[:, :], w["spread"]),
                (la[:, :, :], w["lora_a"].rearrange("j r d -> r j d")),
                (lb[:, :, :], w["lora_b"].rearrange("j r o -> r j o")),
                (brow[:, :, :], w["biases"].rearrange("(m e) o -> e m o", e=2)[0].partition_broadcast(P)),
                (ident[:, :], w["constants"][:, C_IDENT:C_IDENT + P]),
                (rowself[:, :], w["rowsel"]),
                (gamma[:, :, :], w["gamma"].rearrange("m p k -> p m k")),
                (beta[:, :, :], w["beta"].rearrange("m p k -> p m k")),
            ]
            for m in range(BLOCKS):
                loads.append((bias[:, m, :], w["bias_columns"][2 * m + 1]))
            assert len(loads) == N_LOADS - 1
            for to, of in loads:
                sp.dma_start(to, of).then_inc(loaded, 16)

        LOADED = 16 * (N_LOADS - 1)

        @block.tensor
        def _(pe):
            pe.wait_ge(loaded, LOADED)
            for j in range(N):
                wait(pe, full_done, j - 1)
                for kd in range(KD):
                    nc.tensor.matmul(scale_ps[j % 2][:, kd, :], spread[:, kd * P:(kd + 1) * P], scales[:, j, :], start=True, stop=True)
                    last = nc.tensor.matmul(lora_ps[j % 2][:, kd, :], la[:, j, kd * P:(kd + 1) * P], lb[:, j, :], start=True, stop=True)
                last.then_inc(spreadout, 1)

        @block.vector
        def _(dve):
            nc.vector.memset(power[:, :], -0.5)
            dve.wait_ge(loaded, LOADED)
            nc.vector.tensor_scalar(steps[:, :, :, :], q[:, :, :, :], 1.0 / 7.5, -1.0, ALU.mult, ALU.add).then_inc(stepped, 1)
            dve.wait_ge(stepped, 1)
            for j in range(N):
                dve.wait_ge(spreadout, j + 1)
                nc.vector.tensor_tensor(scaled[:, j % 2, :, :], steps[:, j, :, :], scale_ps[j % 2][:, :, :], ALU.mult).then_inc(scaled_done, 1)
                dve.wait_ge(scaled_done, j + 1)
                nc.vector.tensor_tensor(full[:, j, :, :], scaled[:, j % 2, :, :], lora_ps[j % 2][:, :, :], ALU.add).then_inc(full_done, 1)
            dve.wait_ge(full_done, N)
            nc.vector.tensor_copy(whi[:, :, :, :], full[:, :, :, :]).then_inc(hi_done, 1)
            dve.wait_ge(hi_done, 1)
            nc.vector.tensor_tensor(wlo[:, :, :, :], full[:, :, :, :], whi[:, :, :, :].bitcast(F32), ALU.subtract)
            left = brow
            for i in range(PARTS):
                nc.vector.tensor_copy(part[i][:, :, :], left[:, :, :]).then_inc(split, 1)
                dve.wait_ge(split, 2 * i + 1)
                nc.vector.tensor_copy(bias3[32 * i:32 * i + 32, :, :], part[i][32 * i:32 * i + 32, :, :])
                if i < PARTS - 1:
                    nc.vector.tensor_tensor(rest[i][:, :, :], left[:, :, :], part[i][:, :, :], ALU.subtract).then_inc(split, 1)
                    dve.wait_ge(split, 2 * i + 2)
                    left = rest[i]
            nc.vector.tensor_copy(rowsel[:, :], rowself[:, :]).then_inc(prepared, 1)
            dve.wait_ge(prepared, 1)


def mlp_items(nc, h, x, out, k):
    whi, wlo, ident, rowsel, bias3, bias, gamma, beta, power = (
        k[n] for n in ("whi", "wlo", "ident", "rowsel", "bias3", "bias", "gamma", "beta", "power"))
    with ExitStack() as ctx:
        def sb(name, shape, dt=F32):
            return [ctx.enter_context(nc.sbuf_tensor(f"M_{name}{s}", shape, dt)) for s in range(2)]

        def sem(name):
            return nc.alloc_semaphore(name=f"M_{name}")

        hin, xin, x1, normed = (sb(n, [P, NB, DM]) for n in ("hin", "xin", "x1", "normed"))
        nrm, outb = sb("nrm", [P, NB, DM]), sb("outb", [P, NB, DM])
        hT, g = sb("hT", [P, KD, W]), sb("g", [P, KD, W])
        hhi, hlo = sb("hhi", [P, KD, W], F32R), sb("hlo", [P, KD, W], F32R)
        ghi, glo = sb("ghi", [P, KD, W], F32R), sb("glo", [P, KD, W], F32R)
        stats, var, rstd, shift = (sb(n, [P, NB, c]) for n, c in (("stats", 6), ("var", 1), ("rstd", 1), ("shift", 1)))
        stats0, var0, rstd0 = (sb(n, [P, NB, c]) for n, c in (("stats0_", 6), ("var0_", 1), ("rstd0_", 1)))
        mom, mom0 = sb("mom", [P, 6, NB]), sb("mom0_", [P, 6, NB])
        lin = [[ctx.enter_context(nc.psum_tensor(f"M_lin{s}{i}", [P, 512], F32)) for i in range(2)] for s in range(2)]
        turn = [[ctx.enter_context(nc.psum_tensor(f"M_turn{s}{i}", [P, 512], F32)) for i in range(2)] for s in range(2)]

        h_in = [sem(f"h_in{s}") for s in range(2)]
        x1_done, n0_stats, n0_mom, n0_var, n0_rstd, n0_done = (sem(n) for n in ("x1_done", "n0_stats", "n0_mom", "n0_var", "n0_rstd", "n0_done"))
        in_turned, in_copied = sem("in_turned"), sem("in_copied")
        h_hi, h_lo = sem("h_hi"), sem("h_lo")
        first_done = sem("first_done")
        b_stats, b_mom, b_var, b_rstd, b_shift = (sem(n) for n in ("b_stats", "b_mom", "b_var", "b_rstd", "b_shift"))
        b_normed = sem("b_normed")
        b_turned, b_gelu, g_hi, g_lo = (sem(n) for n in ("b_turned", "b_gelu", "g_hi", "g_lo"))
        second_done, h_added = sem("second_done"), sem("h_added")
        out_turned, out_added = sem("out_turned"), sem("out_added")
        stored = [sem(f"stored{s}") for s in range(2)]
        PAIRS = ITEMS // 2

        def turn_of(i, s, m):
            return 2 * BLOCKS * i + 2 * m + s

        def over_pairs(eng, step):
            step(0)
            with eng.Fori(1, PAIRS - 1) as i:
                step(i)
            step(PAIRS - 1)

        block = ctx.enter_context(nc.Block())

        @block.sync
        def _(sp):
            def load(i, s):
                wait(sp, x1_done, 2 * (i - 1) + s + 1)
                for to, of in ((hin, h), (xin, x)):
                    sp.dma_start(to[s][:, :, :], item_tokens(of, i, s)).then_inc(h_in[s], 16)

            def step(i):
                if not isinstance(i, int) or i + 1 < PAIRS:
                    for s in range(2):
                        load(i + 1, s)
                for s in range(2):
                    sp.wait_ge(out_added, 2 * (2 * i + s) + 2)
                    sp.dma_start(item_tokens(out, i, s), outb[s][:, :, :]).then_inc(stored[s], 16)

            for s in range(2):
                load(0, s)
            over_pairs(sp, step)
            for s in range(2):
                sp.wait_ge(stored[s], 16 * PAIRS)

        @block.tensor
        def _(pe):
            def turn_in(i, s):
                n = 2 * i + s
                pe.wait_ge(n0_done, n + 1)
                wait(pe, b_gelu, 2 * turn_of(i, 0, 0))
                for kd in range(KD):
                    for b in range(NB):
                        last = nc.tensor.transpose(turn[s][kd][:, b * P:(b + 1) * P], normed[s][:, b, kd * P:(kd + 1) * P], ident[:, :])
                    last.then_inc(in_turned, 1)

            def first_linear(i, s, m):
                n = turn_of(i, s, m)
                pe.wait_ge(h_lo, 2 * n + 2)
                if m == 0:
                    wait(pe, out_added, 2 * (2 * i + s - 1))
                for b in range(NB):
                    to = lin[s][b // 2][:, (b % 2) * DM:(b % 2 + 1) * DM]
                    nc.tensor.matmul(to, rowsel[:, :], bias3[:, m, :], start=True, stop=False, skip_group_check=True)
                    passes = [(kd, a, ww) for kd in range(KD) for a, ww in ((hhi, whi), (hhi, wlo), (hlo, whi))]
                    for j, (kd, a, ww) in enumerate(passes):
                        last = nc.tensor.matmul(to, a[s][:, kd, b * P:(b + 1) * P], ww[:, 2 * m, kd, :],
                                                start=False, stop=j == len(passes) - 1, skip_group_check=True)
                    if b % 2:
                        last.then_inc(first_done, 1)

            def turn_normed(i, s, m):
                n = turn_of(i, s, m)
                pe.wait_ge(b_normed, n + 1)
                for kd in range(KD):
                    for b in range(NB):
                        last = nc.tensor.transpose(turn[s][kd][:, b * P:(b + 1) * P], nrm[s][:, b, kd * P:(kd + 1) * P], ident[:, :])
                    last.then_inc(b_turned, 1)

            def second_linear(i, s, m):
                n = turn_of(i, s, m)
                pe.wait_ge(g_lo, 2 * n + 2)
                for o in range(KD):
                    passes = [(kd, ww, a) for kd in range(KD) for ww, a in ((whi, ghi), (wlo, ghi), (whi, glo))]
                    for j, (kd, ww, a) in enumerate(passes):
                        last = nc.tensor.matmul(lin[s][o][:, :], ww[:, 2 * m + 1, kd, o * P:(o + 1) * P], a[s][:, kd, :],
                                                start=j == 0, stop=j == len(passes) - 1)
                    last.then_inc(second_done, 1)

            def turn_out(i, s):
                n = turn_of(i, s, BLOCKS - 1)
                pe.wait_ge(h_added, 2 * n + 2)
                for b in range(NB):
                    for kd in range(KD):
                        last = nc.tensor.transpose(lin[s][b // 2][:, (b % 2) * DM + kd * P:(b % 2) * DM + (kd + 1) * P],
                                                   hT[s][:, kd, b * P:(b + 1) * P], ident[:, :])
                    if b % 2:
                        last.then_inc(out_turned, 1)

            def step(i):
                for s in range(2):
                    turn_in(i, s)
                for m in range(BLOCKS):
                    for s in range(2):
                        first_linear(i, s, m)
                    for s in range(2):
                        turn_normed(i, s, m)
                    for s in range(2):
                        second_linear(i, s, m)
                for s in range(2):
                    turn_out(i, s)

            over_pairs(pe, step)

        @block.scalar
        def _(act):
            def copy_in(i, s):
                n = 2 * i + s
                wait(act, out_turned, 2 * (n - 1))
                for kd in range(KD):
                    act.wait_ge(in_turned, 2 * n + kd + 1)
                    nc.scalar.activation(hT[s][:, kd, :], turn[s][kd][:, :], ACT.Copy).then_inc(in_copied, 1)

            def round_h(i, s, m):
                n = turn_of(i, s, m)
                for kd in range(KD):
                    if m == 0:
                        act.wait_ge(in_copied, 2 * (2 * i + s) + kd + 1)
                    else:
                        act.wait_ge(h_added, 2 * turn_of(i, s, m - 1) + kd + 1)
                    nc.scalar.activation(hhi[s][:, kd, :], hT[s][:, kd, :], ACT.Copy).then_inc(h_hi, 1)

            def normalise(i, s, m):
                n = turn_of(i, s, m)
                act.wait_ge(b_shift, n + 1)
                for b in range(NB):
                    last = nc.scalar.activation(nrm[s][:, b, :], lin[s][b // 2][:, (b % 2) * DM:(b % 2 + 1) * DM], ACT.Identity,
                                                bias=shift[s][:, b, :], scale=rstd[s][:, b, :])
                last.then_inc(b_normed, 1)

            def gelu(i, s, m):
                n = turn_of(i, s, m)
                for kd in range(KD):
                    act.wait_ge(b_turned, 2 * n + kd + 1)
                    nc.scalar.activation(g[s][:, kd, :], turn[s][kd][:, :], ACT.Gelu,
                                         bias=beta[:, m, kd:kd + 1], scale=gamma[:, m, kd:kd + 1]).then_inc(b_gelu, 1)
                for kd in range(KD):
                    act.wait_ge(b_gelu, 2 * n + kd + 1)
                    nc.scalar.activation(ghi[s][:, kd, :], g[s][:, kd, :], ACT.Copy).then_inc(g_hi, 1)

            def step(i):
                for s in range(2):
                    copy_in(i, s)
                    round_h(i, s, 0)
                for m in range(BLOCKS):
                    for s in range(2):
                        normalise(i, s, m)
                    for s in range(2):
                        gelu(i, s, m)
                    if m + 1 < BLOCKS:
                        for s in range(2):
                            round_h(i, s, m + 1)

            over_pairs(act, step)

        @block.gpsimd
        def _(pool):
            def rsqrt(out, in_, ready, n, done):
                pool.wait_ge(ready, n + 1)
                nc.gpsimd.tensor_tensor(out[:, :, 0], in_[:, :, 0], power[:, :], ALU.pow).then_inc(done, 1)

            def step(i):
                for m in range(BLOCKS):
                    for s in range(2):
                        rsqrt(rstd[s], var[s], b_var, turn_of(i, s, m), b_rstd)
                if not isinstance(i, int) or i + 1 < PAIRS:
                    for s in range(2):
                        rsqrt(rstd0[s], var0[s], n0_var, 2 * (i + 1) + s, n0_rstd)

            for s in range(2):
                rsqrt(rstd0[s], var0[s], n0_var, s, n0_rstd)
            over_pairs(pool, step)

        @block.vector
        def _(dve):
            def statistics(n, tiles, stats, mom, var, s_stats, s_mom, s_var):
                moments(nc, dve, tiles, stats, mom, var[:, :, 0], s_stats, s_mom, s_var, n)

            def add_x(i, s):
                n = 2 * i + s
                dve.wait_ge(h_in[s], 32 * (i + 1))
                wait(dve, out_added, 2 * (2 * i + s - 1))
                nc.vector.tensor_tensor(x1[s][:, :, :], hin[s][:, :, :], xin[s][:, :, :], ALU.add).then_inc(x1_done, 1)
                dve.wait_ge(x1_done, n + 1)
                statistics(n, [x1[s][:, b, :] for b in range(NB)], stats0[s], mom0[s], var0[s], n0_stats, n0_mom, n0_var)

            def norm_in(i, s):
                n = 2 * i + s
                dve.wait_ge(n0_rstd, n + 1)
                dve.wait_ge(n0_mom, 6 * n + 6)
                for b in range(NB):
                    last = nc.vector.tensor_scalar(normed[s][:, b, :], x1[s][:, b, :], mom0[s][:, 5, b:b + 1], rstd0[s][:, b, :], ALU.subtract, ALU.mult)
                last.then_inc(n0_done, 1)

            def rest_h(i, s, m):
                n = turn_of(i, s, m)
                for kd in range(KD):
                    dve.wait_ge(h_hi, 2 * n + kd + 1)
                    nc.vector.tensor_tensor(hlo[s][:, kd, :], hT[s][:, kd, :], hhi[s][:, kd, :].bitcast(F32), ALU.subtract).then_inc(h_lo, 1)

            def block_stats(i, s, m):
                n = turn_of(i, s, m)
                dve.wait_ge(first_done, 2 * n + 2)
                statistics(n, [lin[s][b // 2][:, (b % 2) * DM:(b % 2 + 1) * DM] for b in range(NB)], stats[s], mom[s], var[s], b_stats, b_mom, b_var)

            def block_shift(i, s, m):
                n = turn_of(i, s, m)
                dve.wait_ge(b_rstd, n + 1)
                dve.wait_ge(b_mom, 6 * n + 6)
                nc.vector.scalar_tensor_tensor(shift[s][:, :, 0], mom[s][:, 5, :], -1.0, rstd[s][:, :, 0], ALU.mult, ALU.mult).then_inc(b_shift, 1)

            def rest_g(i, s, m):
                n = turn_of(i, s, m)
                for kd in range(KD):
                    dve.wait_ge(g_hi, 2 * n + kd + 1)
                    nc.vector.tensor_tensor(glo[s][:, kd, :], g[s][:, kd, :], ghi[s][:, kd, :].bitcast(F32), ALU.subtract).then_inc(g_lo, 1)

            def add_h(i, s, m):
                n = turn_of(i, s, m)
                for kd in range(KD):
                    dve.wait_ge(second_done, 2 * n + kd + 1)
                    nc.vector.scalar_tensor_tensor(hT[s][:, kd, :], lin[s][kd][:, :], bias[:, m, kd:kd + 1], hT[s][:, kd, :], ALU.add, ALU.add).then_inc(h_added, 1)

            def add_out(i, s):
                n = 2 * i + s
                wait(dve, stored[s], 16 * i)
                for j in range(2):
                    dve.wait_ge(out_turned, 2 * n + j + 1)
                    nc.vector.tensor_tensor(outb[s][:, 2 * j:2 * j + 2, :], lin[s][j][:, :].rearrange("p (b d) -> p b d", b=2),
                                            x1[s][:, 2 * j:2 * j + 2, :], ALU.add).then_inc(out_added, 1)

            def step(i):
                for s in range(2):
                    rest_h(i, s, 0)
                for m in range(BLOCKS):
                    for s in range(2):
                        block_stats(i, s, m)
                    for s in range(2):
                        block_shift(i, s, m)
                    for s in range(2):
                        rest_g(i, s, m)
                    for s in range(2):
                        add_h(i, s, m)
                    if m + 1 < BLOCKS:
                        for s in range(2):
                            rest_h(i, s, m + 1)
                for s in range(2):
                    add_out(i, s)
                if not isinstance(i, int) or i + 1 < PAIRS:
                    for s in range(2):
                        add_x(i + 1, s)
                    for s in range(2):
                        norm_in(i + 1, s)

            for s in range(2):
                add_x(0, s)
            for s in range(2):
                norm_in(0, s)
            over_pairs(dve, step)


OUTPUT = ((SEQ, LEN, DM), "float32")


def program(nc, x, out, w):
    h = [nc.dram_tensor(f"h{i}", [SEQ, LEN, DM], F32, kind="Internal").ap() for i in range(2)]
    for phase in (
            lambda: mamba_layer(nc, 0, True, x, h[0], w),
            lambda: mamba_layer(nc, 1, False, h[0], h[1], w),
            lambda: mlp(nc, h[1], x, out, w)):
        with nc.cleanup_on_exit():
            phase()


def laid_out(inputs):
    spread = np.zeros((DM // QGROUP, DM), np.float32)
    spread[np.arange(DM) // QGROUP, np.arange(DM)] = 1
    rowsel = np.zeros((PARTS * 32, P), np.float32)
    rowsel[::32] = 1
    a = {n.split("_", 2)[2]: np.asarray(v) for n, v in inputs.items()}

    def swap(v):
        return v.transpose(0, 2, 1)

    def columns(v, rows=P):
        return swap(v.reshape(v.shape[0], -1, rows))

    arrays = {
        "x": a["x"], "ln_w": columns(a["ln_w"]), "ln_b": columns(a["ln_b"]), "in_proj": swap(a["in_proj_w"]), "conv_w": a["conv_w"],
        "conv_b": columns(a["conv_b"]), "dt_bias": a["dt_bias"], "A_log": a["A_log"], "D": columns(a["D"], 2), "rms_w": columns(a["rms_w"]),
        "out_proj": swap(a["out_proj_w"]), "qweights": swap(a["qweights"]), "scales": swap(a["scales"]), "biases": a["biases"],
        "lora_a": a["lora_a"], "lora_b": swap(a["lora_b"]), "gamma": columns(a["ln_gamma"]), "beta": columns(a["ln_beta"]),
        "bias_columns": columns(a["biases"]),
        "constants": constants(), "spread": spread, "rowsel": rowsel,
    }
    return {f"in_{n}": np.ascontiguousarray(v) for n, v in arrays.items()}


def kernel(**inputs):
    import concourse.bacc as bacc
    from concourse.bass_utils import run_bass_kernel_spmd

    arrays = laid_out(inputs)
    nc = bacc.Bacc("TRN2", target_bir_lowering=False, num_devices=1)
    w = {n[3:]: nc.dram_tensor(n, v.shape, mybir.dt.from_np(v.dtype), kind="ExternalInput").ap() for n, v in arrays.items()}
    out = nc.dram_tensor("out", OUTPUT[0], F32, kind="ExternalOutput").ap()
    program(nc, w["x"], out, w)
    result = run_bass_kernel_spmd(nc, [arrays], core_ids=[0])
    return result.results[0]["out"]
```

```python
from contextlib import ExitStack

import numpy as np

import concourse.bass as bass
from concourse import mybir

F32 = mybir.dt.float32
F32R = mybir.dt.float32r
BF16 = mybir.dt.bfloat16
I32 = mybir.dt.int32
ALU = mybir.AluOpType
ACT = mybir.ActivationFunctionType

P = 128
DM = 256
KD = DM // P
DI = 512
T = DI // P
NH = 8
HD = 64
NS = 64
TAPS = 4
NPROJ = 2 * DI + 2 * NS + NH
SEQ, LEN = 8, 1024
CHUNKS = LEN // P
NB = 4
GROUPS = SEQ // NB
ITEMS = CHUNKS * GROUPS
W = NB * P
HALO = TAPS - 1
EPS = 1e-5
QCONV = T + 1
PARTS = 3
ROWS = 64
BLOCKS = 3
RANK = 32
QGROUP = 16

LAYERS = 2

C_IDENT, C_TRI, C_SUF, C_COL, C_MASK = 0, P, 2 * P, 3 * P, 3 * P + 4
C_SEL = C_MASK + NH * P
C_END = C_SEL + 2 * P

VECTORS = {"ln_w": KD, "ln_b": KD, "rms_w": T, "conv_w": QCONV * TAPS, "conv_b": QCONV, "dt_bias": NH, "A_log": NH, "D": T}
V_AT = {n: sum(list(VECTORS.values())[:i]) for i, n in enumerate(VECTORS)}
V_END = sum(VECTORS.values())


def constants():
    c = np.zeros((P, C_END), np.float32)
    i = np.arange(P)
    c[:, C_IDENT:C_IDENT + P] = np.eye(P)
    c[:, C_TRI:C_TRI + P] = i[:, None] <= i[None, :]
    c[:, C_SUF:C_SUF + P] = i[:, None] > i[None, :]
    for half in range(2):
        for dup in range(2):
            for part in range(PARTS):
                for h in range(NH):
                    row = ROWS * half + PARTS * NH * dup + NH * part + h
                    c[row, C_MASK + h * P:C_MASK + (h + 1) * P] = -1 if dup else 1
                    if not dup:
                        odd = h % 2
                        at = C_SEL + P * odd + HD * odd
                        c[row, at:at + HD] = 1
                    c[row, C_COL + 0] = dup
                    c[row, C_COL + 1] = 1 - dup
                    c[row, C_COL + 2] = 1 - dup
                    c[row, C_COL + 3] = dup
    return c


def wait(eng, sem, value):
    if isinstance(value, int) and value <= 0:
        return
    eng.wait_ge(sem, value)


def over_items(eng, step):
    for layer in range(LAYERS):
        for p in range(2):
            step(ITEMS * layer + p, layer, 0, p)
        with eng.Fori(0, CHUNKS - 2) as i:
            for p in range(2):
                step(2 * i + (ITEMS * layer + 2 + p), layer, i + 1, p)
        for p in range(2):
            step(ITEMS * layer + ITEMS - 2 + p, layer, CHUNKS - 1, p)


def follows(n, by):
    return not isinstance(n, int) or n + by < LAYERS * ITEMS


def layer_of(n, layer, by):
    return (n + by) // ITEMS if isinstance(n, int) else layer


def follows_any(n):
    return not isinstance(n, int) or n > 0


def starts_layer(n):
    return isinstance(n, int) and n % ITEMS == 0 and n < LAYERS * ITEMS


def ends_sequence(n):
    return isinstance(n, int) and n % ITEMS >= ITEMS - GROUPS


MOMENTS = ("sum2", "gap", "within", "gap2", "spread", "mean")


def moments(nc, dve, tiles, stats, mom, var, s_stats, s_mom, s_var, n, sign=1, ready=lambda b: None, factor=1.0, eps=EPS):
    at = {name: mom[:, i, :] for i, name in enumerate(MOMENTS)}
    for b in range(NB):
        ready(b)
        nc.vector.bn_stats(stats[:, b, :], tiles[b]).then_inc(s_stats, 1)
    dve.wait_ge(s_stats, NB * n + NB)
    nc.vector.tensor_tensor(at["gap"], stats[:, :, 1], stats[:, :, 4], ALU.subtract).then_inc(s_mom, 1)
    nc.vector.tensor_tensor(at["within"], stats[:, :, 2], stats[:, :, 5], ALU.add).then_inc(s_mom, 1)
    nc.vector.tensor_tensor(at["sum2"], stats[:, :, 1], stats[:, :, 4], ALU.add).then_inc(s_mom, 1)
    dve.wait_ge(s_mom, 6 * n + 1)
    nc.vector.tensor_tensor(at["gap2"], at["gap"], at["gap"], ALU.mult).then_inc(s_mom, 1)
    dve.wait_ge(s_mom, 6 * n + 4)
    nc.vector.scalar_tensor_tensor(at["spread"], at["gap2"], DM / 4.0, at["within"], ALU.mult, ALU.add).then_inc(s_mom, 1)
    nc.vector.tensor_scalar(at["mean"], at["sum2"], 0.5 * sign, None, ALU.mult).then_inc(s_mom, 1)
    dve.wait_ge(s_mom, 6 * n + 5)
    nc.vector.tensor_scalar(var, at["spread"], factor / DM, eps, ALU.mult, ALU.add).then_inc(s_var, 1)


def item_tokens(dram, chunk, group):
    view = dram.rearrange("(g b) (c p) d -> c g p b d", b=NB, p=P)
    if isinstance(chunk, int):
        return view[chunk, group]
    return view[bass.ds(chunk, 1), group].rearrange("a p b d -> (a p) b d")


def mamba_layers(nc, x, h, out, w):
    with ExitStack() as ctx:
        def sb(name, shape, dt=F32):
            return ctx.enter_context(nc.sbuf_tensor(f"L_{name}", shape, dt))

        def bank(name):
            return ctx.enter_context(nc.psum_tensor(f"L_{name}", [P, 512], F32))

        def sem(name):
            return nc.alloc_semaphore(name=f"L_{name}")

        src, dst = (x, h), (h, out)

        kept = sb("kept", [P, C_MASK])
        ident, tri, suffix = (kept[:, c:c + P] for c in (C_IDENT, C_TRI, C_SUF))
        col = kept[:, C_COL:C_COL + 4]
        identb, mask, sel = sb("identb", [P, P], BF16), sb("mask", [P, NH, P], BF16), sb("sel", [P, 2, P], BF16)
        ones, power = sb("ones", [P, P]), sb("power", [P, NB])
        vec = sb("vec", [P, LAYERS, V_END])

        def vector(layer, name, i=0, n=None):
            return vec[:, layer, V_AT[name] + i:V_AT[name] + (VECTORS[name] if n is None else i + n)]

        raw = sb("raw", [P, KD, NPROJ])
        whi, wlo = sb("whi", [P, KD, NPROJ], F32R), sb("wlo", [P, KD, NPROJ], F32R)
        wo = [sb(f"wo{layer}", [P, T, DM]) for layer in range(LAYERS)]
        lnb_rows = sb("lnb_rows", [P, KD, P])
        pbias = sb("pbias", [P, LAYERS, 2 * T + 1])
        dtb = sb("dtb", [P, LAYERS, NH])
        aexp, aneg = sb("aexp", [P, LAYERS, NH]), sb("aneg", [P, LAYERS, NH])

        hin = [sb(f"hin{p}", [P, NB, DM]) for p in range(2)]
        hres = [sb(f"hres{p}", [P, NB, DM]) for p in range(2)]
        var0, mean0, rstd0 = sb("var0", [P, NB]), [sb(f"mean0_{p}", [P, NB]) for p in range(2)], [sb(f"rstd0_{p}", [P, NB]) for p in range(2)]
        stats, mom, var, rstd, shift = sb("stats", [P, NB, 6]), sb("mom", [P, 6, NB]), sb("var", [P, NB]), sb("rstd", [P, NB]), sb("shift", [P, NB])
        uhi, ulo = sb("uhi", [P, KD, W], F32R), sb("ulo", [P, KD, W], F32R)
        xpad = sb("xpad", [P, QCONV, NB, HALO + P])
        halo = [sb(f"halo{g}", [P, QCONV, NB, HALO]) for g in range(GROUPS)]
        xc = [sb(f"xc{p}", [P, QCONV, W]) for p in range(2)]
        cc = sb("cc", [P, W])
        sz = sb("sz", [P, T, W])
        dtT = sb("dtT", [P, W])
        dtraw, dtabs, dtexp, dtln = (sb(x, [P, NB, NH]) for x in ("dtraw", "dtabs", "dtexp", "dtln"))
        dtv = [sb(f"dtv{p}", [P, NB, NH]) for p in range(2)]
        da = sb("da", [P, NB, NH])
        sums = sb("sums", [P, 3, NB, NH])
        decay = [sb(f"decay{p}", [P, NB, NH]) for p in range(2)]
        sdecay = [sb(f"sdecay{p}", [P, NB, T]) for p in range(2)]
        rest1, rest2 = sb("rest1", [P, NB, NH]), sb("rest2", [P, NB, NH])
        cum3 = sb("cum3", [P, NB, ROWS], BF16)
        dstat, dmovT = sb("dstat", [P, 2, P], BF16), sb("dmovT", [P, 2, P], BF16)
        dmov = sb("dmov", [P, 2, NH, P], BF16)
        expd = sb("expd", [P, 2, NH // 2, P])
        gm = sb("gm", [P, NB, P])
        m = sb("m", [P, NB, NH, P])
        dtx = sb("dtx", [P, NB, NH, HD])
        wx = sb("wx", [P, NB, NH, HD])
        bt = sb("bt", [P, NB, NS])
        ecum = sb("ecum", [P, 2, T, P])
        cs = sb("cs", [P, NB, T, P])
        state = [sb(f"state{g}", [P, NB, T, HD]) for g in range(GROUPS)]
        sdec = sb("sdec", [P, NB, T, HD])
        yg = sb("yg", [P, T, W])
        sq = sb("sq", [P, T, W])
        ssq, rrms = sb("ssq", [P, NB]), sb("rrms", [P, NB])
        front = [bank(f"front{i}") for i in range(2)]
        dbank = [bank(f"dbank{i}") for i in range(2)]
        ybank = [bank(f"ybank{i}") for i in range(2)]
        mix = [bank(f"mix{i}") for i in range(2)]
        staged = m[:, :, :, :].rearrange("p b h i -> p (b h i)")[:, 0:C_END - C_MASK]
        BIAS_AT = NB

        h_in = [sem(f"h_in{p}") for p in range(2)]
        res_in = [sem(f"res_in{p}") for p in range(2)]
        cc_in = sem("cc_in")
        stored = sem("stored")
        consts_in, vec_in, raw_in, wo_in = (sem(x) for x in ("consts_in", "vec_in", "raw_in", "wo_in"))
        ones_ready, consts_ready, cleared = sem("ones_ready"), sem("consts_ready"), sem("cleared")
        aexp_ready, wo_ready = sem("aexp_ready"), sem("wo_ready")
        rows_ready, hi_ready, lo_ready = sem("rows_ready"), sem("hi_ready"), sem("lo_ready")
        bias_summed, bias_ready = sem("bias_summed"), sem("bias_ready")
        ln0_var, ln0_rstd = sem("ln0_var"), sem("ln0_rstd")
        ln_stats, ln_mom, ln_var, ln_rstd, ln_shift, ln_done = (sem(x) for x in ("ln_stats", "ln_mom", "ln_var", "ln_rstd", "ln_shift", "ln_done"))
        u_turned, u_hi, u_lo = sem("u_turned"), sem("u_hi"), sem("u_lo")
        proj = sem("proj")
        dt_kept, dt_turned = sem("dt_kept"), sem("dt_turned")
        dt_biased, dt_abs, dt_exp, dt_ln, dt_done, da_done = (sem(x) for x in ("dt_biased", "dt_abs", "dt_exp", "dt_ln", "dt_done", "da_done"))
        da_summed, sums_out, decay_done = sem("da_summed"), sem("sums_out"), sem("decay_done")
        split = sem("split")
        cum_turned, dops, dmov_done, dmov2_done = sem("cum_turned"), sem("dops"), sem("dmov_done"), sem("dmov2_done")
        halo_set, halo_kept, halo_cleared = sem("halo_set"), sem("halo_kept"), sem("halo_cleared")
        x_raw, tap0, taps, conved = sem("x_raw"), sem("tap0"), sem("taps"), sem("conved")
        z_done = sem("z_done")
        g_done, gm_done = sem("g_done"), sem("gm_done")
        d_ready, d_abs, d_exp, m_done = sem("d_ready"), sem("d_abs"), sem("d_exp"), sem("m_done")
        xt_done, dtx_done, wx_done = sem("xt_done"), sem("dtx_done"), sem("wx_done")
        bt_turned, bt_done = sem("bt_turned"), sem("bt_done")
        ec_ready, ec_exp, cs_done = sem("ec_ready"), sem("ec_exp"), sem("cs_done")
        st_ready, sdec_done, state_done = sem("st_ready"), sem("sdec_done"), sem("state_done")
        y_ready, y_skip, y_gated, y_sq = sem("y_ready"), sem("y_skip"), sem("y_gated"), sem("y_sq")
        sq_added = sem("sq_added")
        ss_ready, ss_done, rr_done = sem("ss_ready"), sem("ss_done"), sem("rr_done")
        res_normed = sem("res_normed")
        o_ready, h_done = sem("o_ready"), sem("h_done")

        QORDER = [T, 0, 1, 2, 3]
        N_PROJ = 1 + QCONV + T

        block = ctx.enter_context(nc.Block())

        @block.sync
        def _(sp):
            def load_in(n, layer, c, p):
                wait(sp, u_turned, KD * (n - 1))
                if layer > 0 and isinstance(n, int) and n < ITEMS + GROUPS + 1:
                    sp.wait_ge(stored, 16 * (n - ITEMS + 1))
                sp.dma_start(hin[p][:, :, :], item_tokens(src[layer], c, p)).then_inc(h_in[p], 16)

            def load_res(n, layer, c, p):
                wait(sp, stored, 16 * (n - 1))
                sp.dma_start(hres[p][:, :, :], item_tokens(src[layer], c, p)).then_inc(res_in[p], 16)

            def store(n, layer, c, p):
                sequences = dst[layer].rearrange("(g b) s d -> g s b d", b=NB)
                sp.wait_ge(h_done, NB * (n + 1))
                sp.dma_start(sequences[p, bass.ds(c * P, P)], hres[p][:, :, :]).then_inc(stored, 16)

            def step(n, layer, c, p):
                if follows(n, 2):
                    load_in(n + 2, layer_of(n, layer, 2), 0 if ends_sequence(n) else c + 1, p)
                if follows_any(n):
                    store(n - 1, layer_of(n, layer, -1), CHUNKS - 1 if starts_layer(n) else c if p else c - 1, 1 - p)
                    if follows(n, 1):
                        load_res(n + 1, layer_of(n, layer, 1), 0 if starts_layer(n + 1) else c + 1 if p else c, 1 - p)
                if isinstance(n, int) and n == ITEMS:
                    sp.wait_ge(stored, 16 * ITEMS)

            load_in(0, 0, 0, 0)
            sp.dma_start(kept[:, :], w["constants"][:, 0:C_MASK]).then_inc(consts_in, 16)
            sp.dma_start(vec[:, :, :], w["vectors"]).then_inc(vec_in, 16)
            sp.dma_start(staged, w["constants"][:, C_MASK:C_END]).then_inc(consts_in, 16)
            load_in(1, 0, 0, 1)
            for p in range(2):
                load_res(p, 0, 0, p)
            sp.wait_ge(lo_ready, KD)
            sp.wait_ge(bias_summed, 1)
            sp.dma_start(raw[:, :, :], w["in_proj"][1].rearrange("(k p) n -> p k n", p=P)).then_inc(raw_in, 16)
            over_items(sp, step)
            store(LAYERS * ITEMS - 1, LAYERS - 1, CHUNKS - 1, 1)
            sp.wait_ge(stored, 16 * LAYERS * ITEMS)

        @block.tensor
        def _(pe):
            def turn_u(n, p):
                pe.wait_ge(ln_done, n + 1)
                wait(pe, z_done, T * n)
                for kd in range(KD):
                    for b in range(NB):
                        last = nc.tensor.transpose(front[kd][:, b * P:(b + 1) * P], hin[p][:, b, kd * P:(kd + 1) * P], ident[:, :])
                    last.then_inc(u_turned, 1)

            def fold_bias(layer):
                pe.wait_ge(raw_in, 16 * (layer + 1))
                if layer == 0:
                    pe.wait_ge(vec_in, 16)
                else:
                    pe.wait_ge(ss_done, ITEMS * layer - 1)
                for ct in range(2 * T + 1):
                    for kd in range(KD):
                        nc.tensor.matmul(ybank[1][:, BIAS_AT + ct:BIAS_AT + ct + 1], raw[:, kd, ct * P:(ct + 1) * P], vector(layer, "ln_b", kd, 1),
                                         start=kd == 0, stop=kd == KD - 1)
                pe.wait_ge(rows_ready, KD * (layer + 1))
                at = BIAS_AT + 2 * T + 1
                for kd in range(KD):
                    last = nc.tensor.matmul(ybank[1][:, at:at + NH], lnb_rows[:, kd, :], raw[:, kd, NPROJ - NH:NPROJ],
                                            start=kd == 0, stop=kd == KD - 1)
                last.then_inc(bias_summed, 1)

            def project_dt(n):
                if starts_layer(n):
                    pe.wait_ge(lo_ready, KD * (n // ITEMS + 1))
                pe.wait_ge(u_lo, KD * n + KD)
                passes = [(kd, a, ww) for kd in range(KD) for ww, a in ((whi, uhi), (whi, ulo), (wlo, uhi))]
                for i, (kd, a, ww) in enumerate(passes):
                    last = nc.tensor.matmul(front[0][0:NH, :], ww[:, kd, NPROJ - NH:NPROJ], a[:, kd, :],
                                            start=i == 0, stop=i == len(passes) - 1)
                last.then_inc(proj, 1)

            def turn_dt(n):
                pe.wait_ge(dt_kept, n + 1)
                for b in range(NB):
                    last = nc.tensor.transpose(front[0][:, b * P:(b + 1) * P], dtT[:, b * P:(b + 1) * P], ident[:, :])
                last.then_inc(dt_turned, 1)

            def project(to, tile):
                passes = [(kd, a, ww) for kd in range(KD) for ww, a in ((whi, uhi), (whi, ulo), (wlo, uhi))]
                for i, (kd, a, ww) in enumerate(passes):
                    last = nc.tensor.matmul(to[:, :], ww[:, kd, tile * P:(tile + 1) * P], a[:, kd, :],
                                            start=i == 0, stop=i == len(passes) - 1)
                last.then_inc(proj, 1)

            def project_conv(n, i):
                if i == 0:
                    pe.wait_ge(u_lo, KD * n + KD)
                elif i == 1:
                    pe.wait_ge(dt_biased, n + 1)
                else:
                    pe.wait_ge(x_raw, QCONV * n + i - 1)
                project(front[(i + 1) % 2], T + QORDER[i])

            def sum_da(n):
                pe.wait_ge(da_done, n + 1)
                pe.wait_ge(x_raw, QCONV * n + 4)
                for i, matrix in enumerate((tri, suffix, ones)):
                    last = nc.tensor.matmul(front[0][:, i * NB * NH:(i + 1) * NB * NH], matrix[:, :],
                                            da[:, :, :].rearrange("p b h -> p (b h)"), start=True, stop=True)
                last.then_inc(da_summed, 1)

            def turn_cum(n):
                pe.wait_ge(x_raw, QCONV * n + 5)
                pe.wait_ge(split, 5 * n + 5)
                for pair in range(2):
                    last = nc.tensor.transpose(front[1][:, pair * P // 2:(pair + 1) * P // 2].bitcast(BF16),
                                               cum3[:, 2 * pair:2 * pair + 2, :].rearrange("p b r -> p (b r)"), identb[:, :])
                last.then_inc(cum_turned, 1)

            def project_z(n, t):
                if t == 0:
                    pe.wait_ge(sums_out, n + 1)
                elif t == 1:
                    pe.wait_ge(dops, 2 * n + 2)
                else:
                    pe.wait_ge(z_done, T * n + t - 1)
                project(front[t % 2], t)

            def scores(n, p):
                pe.wait_ge(cc_in, 32 * (n + 1))
                wait(pe, y_skip, T * n)
                for b in range(NB):
                    last = nc.tensor.matmul(ybank[0][:, b * P:(b + 1) * P], xc[p][0:NS, T, b * P:(b + 1) * P],
                                            cc[0:NS, b * P:(b + 1) * P], start=True, stop=True)
                last.then_inc(g_done, 1)

            def decays(n, q):
                b, half = q // 2, q % 2
                if q == 0:
                    pe.wait_ge(dmov_done, n + 1)
                elif q == 4:
                    pe.wait_ge(dmov2_done, n + 1)
                wait(pe, d_abs, 8 * n + q - 1)
                rows = slice(ROWS * (b % 2), ROWS * (b % 2) + ROWS)
                nc.tensor.matmul(dbank[half][:, :], dstat[rows, b // 2, :],
                                 dmov[rows, b // 2, 4 * half:4 * half + 4, :], start=True, stop=True).then_inc(d_ready, 1)

            def turn_x(n, p, b):
                if b == 0:
                    pe.wait_ge(conved, QCONV * n + QCONV)
                    wait(pe, h_done, NB * n - NB // 2)
                elif b == 1:
                    wait(pe, h_done, NB * n)
                else:
                    pe.wait_ge(dtx_done, NB * n + b - 1)
                for t in range(T):
                    last = nc.tensor.transpose(mix[(b + 1) % 2][:, t * P:(t + 1) * P], xc[p][:, t, b * P:(b + 1) * P], ident[:, :])
                last.then_inc(xt_done, 1)

            def turn_b(n, p):
                pe.wait_ge(dtx_done, NB * n + 3)
                for b in range(NB):
                    last = nc.tensor.transpose(mix[1][:, b * P:(b + 1) * P], xc[p][:, T, b * P:(b + 1) * P], ident[:, :])
                last.then_inc(bt_turned, 1)

            def carry(n, b):
                if b == 0:
                    pe.wait_ge(dtx_done, NB * n + 4)
                elif b == 1:
                    pe.wait_ge(bt_done, n + 1)
                else:
                    pe.wait_ge(ec_exp, NB * n + b - 1)
                rows = slice(ROWS * (b % 2), ROWS * (b % 2) + ROWS)
                moving = dmov[rows, b // 2, :, :].rearrange("r (t o) i -> r t o i", o=2)
                for odd in range(2):
                    last = nc.tensor.matmul(mix[b % 2][:, :], sel[rows, odd, :], moving[:, :, odd, :], start=odd == 0, stop=odd == 1)
                last.then_inc(ec_ready, 1)

            def new_state(n, s):
                pe.wait_ge(ec_exp, NB * n + 3 + s)
                pe.wait_ge(wx_done, NB * n + 2 * s + 2)
                pe.wait_ge(bt_done, n + 1)
                for b in (2 * s, 2 * s + 1):
                    values = wx[:, b, :, :].rearrange("p (t o) d -> p t o d", o=2)
                    for odd in range(2):
                        last = nc.tensor.matmul(mix[s][HD * odd:HD * odd + HD, (b % 2) * T * HD:(b % 2 + 1) * T * HD],
                                                bt[:, b, :], values[:, :, odd, :], start=True, stop=True)
                last.then_inc(st_ready, 1)

            def outputs(n, p, t):
                if t == 0:
                    pe.wait_ge(m_done, 8 * n + 8)
                    wait(pe, state_done, 2 * (n - 1))
                    if isinstance(n, int) and n < GROUPS:
                        pe.wait_ge(cleared, 1)
                wait(pe, y_skip, T * n + t - 1)
                to = ybank[t % 2]
                for b in range(NB):
                    at = slice(b * P, (b + 1) * P)
                    if t == 0:
                        pe.wait_ge(cs_done, NB * n + b + 1)
                    for odd in range(2):
                        half = slice(HD * odd, HD * odd + HD)
                        nc.tensor.matmul(to[half, at], dtx[:, b, 2 * t + odd, :], m[:, b, 2 * t + odd, :],
                                         start=True, stop=False, skip_group_check=True)
                    for odd in range(2):
                        half = slice(HD * odd, HD * odd + HD)
                        last = nc.tensor.matmul(to[half, at], state[p][half, b, t, :], cs[half, b, t, :],
                                                start=False, stop=True, skip_group_check=True)
                last.then_inc(y_ready, 1)

            def square_sums(n):
                pe.wait_ge(sq_added, (T - 1) * (n + 1))
                for b in range(NB):
                    last = nc.tensor.matmul(ybank[1][:, b:b + 1], sq[:, 0, b * P:(b + 1) * P], ones[:, 0:1], start=True, stop=True)
                last.then_inc(ss_ready, 1)

            def result(n, layer, s):
                if s == 0:
                    if starts_layer(n):
                        pe.wait_ge(wo_ready, layer + 1)
                    pe.wait_ge(y_gated, T * n + T)
                    pe.wait_ge(state_done, 2 * n + 2)
                for b in (2 * s, 2 * s + 1):
                    for t in range(T):
                        last = nc.tensor.matmul(mix[1 - s][:, (b % 2) * DM:(b % 2 + 1) * DM], yg[:, t, b * P:(b + 1) * P],
                                                wo[layer][:, t, :], start=t == 0, stop=t == T - 1)
                last.then_inc(o_ready, 1)

            def front_part(n, p):
                pe.wait_ge(consts_in, 32)
                turn_u(n, p)
                fold_bias(0)
                project_dt(n)
                project_conv(n, 0)
                turn_dt(n)
                for i in range(1, QCONV):
                    project_conv(n, i)
                sum_da(n)
                pe.wait_ge(consts_ready, 3)
                turn_cum(n)
                for t in range(T):
                    project_z(n, t)
                start_scan(n, p)
                turn_u(n + 1, 1 - p)
                decays(n, 2)
                project_dt(n + 1)
                decays(n, 3)

            def start_scan(n, p):
                scores(n, p)
                decays(n, 0)
                decays(n, 1)

            def step(n, layer, c, p):
                more, more2 = follows(n, 1), follows(n, 2)
                if more:
                    project_conv(n + 1, 0)
                    turn_dt(n + 1)
                decays(n, 4)
                turn_x(n, p, 0)
                if follows_any(n):
                    result(n - 1, layer_of(n, layer, -1), 1)
                decays(n, 5)
                if more:
                    project_conv(n + 1, 1)
                turn_x(n, p, 1)
                turn_x(n, p, 2)
                decays(n, 6)
                if more:
                    project_conv(n + 1, 2)
                turn_x(n, p, 3)
                turn_b(n, p)
                decays(n, 7)
                carry(n, 0)
                carry(n, 1)
                if more:
                    project_conv(n + 1, 3)
                carry(n, 2)
                carry(n, 3)
                if more:
                    project_conv(n + 1, 4)
                outputs(n, p, 0)
                outputs(n, p, 1)
                if more:
                    sum_da(n + 1)
                outputs(n, p, 2)
                if more:
                    project_z(n + 1, 0)
                    turn_cum(n + 1)
                outputs(n, p, 3)
                if more:
                    project_z(n + 1, 1)
                new_state(n, 0)
                if more:
                    project_z(n + 1, 2)
                new_state(n, 1)
                if more:
                    project_z(n + 1, 3)
                    start_scan(n + 1, 1 - p)
                if more2:
                    turn_u(n + 2, p)
                result(n, layer, 0)
                if more:
                    decays(n + 1, 2)
                square_sums(n)
                if starts_layer(n + 2):
                    fold_bias(layer_of(n, layer, 2))
                if more2:
                    project_dt(n + 2)
                if more:
                    decays(n + 1, 3)

            front_part(0, 0)
            over_items(pe, step)
            result(LAYERS * ITEMS - 1, LAYERS - 1, 1)

        @block.scalar
        def _(act):
            def norm(n, p):
                act.wait_ge(ln_shift, n + 1)
                for b in range(NB):
                    last = nc.scalar.activation(hin[p][:, b, :], hin[p][:, b, :], ACT.Identity, bias=shift[:, b:b + 1], scale=rstd[:, b:b + 1])
                last.then_inc(ln_done, 1)

            def round_u(n):
                for kd in range(KD):
                    act.wait_ge(u_turned, KD * n + kd + 1)
                    if kd == 0:
                        wait(act, proj, N_PROJ * n)
                    nc.scalar.activation(uhi[:, kd, :], front[kd][:, :], ACT.Copy).then_inc(u_hi, 1)

            def keep_dt(n):
                act.wait_ge(proj, N_PROJ * n + 1)
                if isinstance(n, int) and n == 0:
                    act.wait_ge(ones_ready, 2)
                wait(act, dt_turned, n)
                nc.scalar.activation(dtT[0:NH, :], front[0][0:NH, :], ACT.Copy).then_inc(dt_kept, 1)

            def softplus(n):
                act.wait_ge(dt_biased, n + 1)
                nc.scalar.activation(dtabs[:, :, :], dtraw[:, :, :], ACT.Abs).then_inc(dt_abs, 1)
                act.wait_ge(dt_abs, n + 1)
                nc.scalar.activation(dtexp[:, :, :], dtabs[:, :, :], ACT.Exp, scale=-1.0).then_inc(dt_exp, 1)
                act.wait_ge(dt_exp, n + 1)
                nc.scalar.activation(dtln[:, :, :], dtexp[:, :, :], ACT.Ln, bias=1.0).then_inc(dt_ln, 1)

            def raw_conv(n, layer, p, i):
                q = QORDER[i]
                act.wait_ge(proj, N_PROJ * n + 2 + i)
                wait(act, taps, 3 * QCONV * n)
                if i == 0:
                    wait(act, halo_kept, n)
                    if starts_layer(n):
                        act.wait_ge(bias_ready, layer + 1)
                nc.scalar.activation(xpad[:, q, :, HALO:], front[(i + 1) % 2][:, :].rearrange("p (b i) -> p b i", b=NB),
                                     ACT.Identity, bias=pbias[:, layer, T + q:T + q + 1]).then_inc(x_raw, 1)
            def silu_conv(n, layer, p, i):
                q = QORDER[i]
                act.wait_ge(taps, 3 * QCONV * n + 3 * i + 3)
                nc.scalar.activation(xc[p][:, q, :], xc[p][:, q, :], ACT.Silu, bias=vector(layer, "conv_b", q, 1)).then_inc(conved, 1)

            def double_c(n, p):
                act.wait_ge(conved, QCONV * n + 1)
                wait(act, cs_done, NB * n)
                wait(act, g_done, n)
                for half in range(2):
                    act.dma_start(cc[half * NS:(half + 1) * NS, :], xc[p][NS:2 * NS, T, :]).then_inc(cc_in, 16)

            def exp_sums(n, p):
                act.wait_ge(sums_out, n + 1)
                wait(act, sdec_done, n - 1)
                nc.scalar.activation(decay[p][:, :, :], sums[:, 1, :, :], ACT.Exp).then_inc(decay_done, 1)
                for odd in range(2):
                    half = slice(HD * odd, HD * odd + HD)
                    nc.scalar.activation(sdecay[p][half, :, :], sums[half, 2, :, :].rearrange("p b (t o) -> p b t o", o=2)[:, :, :, odd],
                                         ACT.Exp).then_inc(decay_done, 1)

            def silu_z(n, layer, t):
                act.wait_ge(proj, N_PROJ * n + 2 + QCONV + t)
                wait(act, y_gated, T * (n - 1) + t + 1)
                nc.scalar.activation(sz[:, t, :], front[t % 2][:, :], ACT.Silu, bias=pbias[:, layer, t:t + 1]).then_inc(z_done, 1)

            def exp_decay(n, q):
                act.wait_ge(d_ready, 8 * n + q + 1)
                wait(act, m_done, 8 * n + q - 1)
                nc.scalar.activation(expd[:, q % 2, :, :], dbank[q % 2][:, :].rearrange("p (h i) -> p h i", i=P), ACT.Abs).then_inc(d_abs, 1)
                act.wait_ge(d_abs, 8 * n + q + 1)
                nc.scalar.activation(expd[:, q % 2, :, :], expd[:, q % 2, :, :], ACT.Exp, scale=-1.0).then_inc(d_exp, 1)

            def keep_b(n):
                act.wait_ge(bt_turned, n + 1)
                wait(act, st_ready, 2 * n)
                nc.scalar.activation(bt[:, :, :], mix[1][:, :].rearrange("p (b c) -> p b c", b=NB)[:, :, 0:NS], ACT.Copy).then_inc(bt_done, 1)

            def exp_carry(n, b):
                act.wait_ge(ec_ready, NB * n + b + 1)
                wait(act, cs_done, NB * n + b - 1)
                nc.scalar.activation(ecum[:, b % 2, :, :], mix[b % 2][:, :].rearrange("p (t i) -> p t i", t=T),
                                     ACT.Exp).then_inc(ec_exp, 1)

            def square(n, t):
                act.wait_ge(y_gated, T * n + t + 1)
                nc.scalar.activation(sq[:, t, :], yg[:, t, :], ACT.Square).then_inc(y_sq, 1)

            def fold_weights(layer):
                act.wait_ge(raw_in, 16 * (layer + 1))
                wait(act, proj, N_PROJ * ITEMS * layer)
                for kd in range(KD):
                    nc.scalar.activation(whi[:, kd, :], raw[:, kd, :], ACT.Copy, scale=vector(layer, "ln_w", kd, 1)).then_inc(hi_ready, 1)

            def front_part(n, p):
                norm(n, p)
                round_u(n)
                fold_weights(0)
                keep_dt(n)
                softplus(n)
                for i in range(QCONV):
                    raw_conv(n, 0, p, i)
                for i in range(QCONV):
                    silu_conv(n, 0, p, i)
                double_c(n, p)
                for t in range(T):
                    silu_z(n, 0, t)
                norm(n + 1, 1 - p)
                start_scan(n, p)
                round_u(n + 1)
                exp_decay(n, 1)
                exp_decay(n, 2)

            def start_scan(n, p):
                exp_sums(n, p)
                exp_decay(n, 0)

            def step(n, layer, c, p):
                more, next_layer = follows(n, 1), layer_of(n, layer, 1)
                if more:
                    keep_dt(n + 1)
                exp_decay(n, 3)
                if more:
                    raw_conv(n + 1, next_layer, 1 - p, 0)
                exp_decay(n, 4)
                exp_decay(n, 5)
                if more:
                    raw_conv(n + 1, next_layer, 1 - p, 1)
                exp_decay(n, 6)
                if more:
                    raw_conv(n + 1, next_layer, 1 - p, 2)
                keep_b(n)
                exp_decay(n, 7)
                for b in range(NB):
                    exp_carry(n, b)
                if more:
                    softplus(n + 1)
                    raw_conv(n + 1, next_layer, 1 - p, 3)
                    raw_conv(n + 1, next_layer, 1 - p, 4)
                    silu_conv(n + 1, next_layer, 1 - p, 0)
                    double_c(n + 1, 1 - p)
                if follows(n, 2):
                    norm(n + 2, p)
                for t in range(T):
                    if more:
                        silu_z(n + 1, next_layer, t)
                    square(n, t)
                    if more:
                        silu_conv(n + 1, next_layer, 1 - p, t + 1)
                if more:
                    start_scan(n + 1, 1 - p)
                if follows(n, 2):
                    round_u(n + 2)
                if more:
                    exp_decay(n + 1, 1)
                    exp_decay(n + 1, 2)
                if follows(n, 2):
                    if starts_layer(n + 2):
                        fold_weights(layer_of(n, layer, 2))

            act.dma_start(raw[:, :, :], w["in_proj"][0].rearrange("(k p) n -> p k n", p=P)).then_inc(raw_in, 16)
            for i in range(LAYERS):
                act.dma_start(wo[i][:, :, :], w["out_proj"][i].rearrange("(t p) n -> p t n", p=P)).then_inc(wo_in, 16)
            act.wait_ge(vec_in, 16)
            nc.scalar.activation(aexp[:, :, :], vec[:, :, V_AT["A_log"]:V_AT["A_log"] + NH], ACT.Exp).then_inc(aexp_ready, 1)
            front_part(0, 0)
            over_items(act, step)

        @block.gpsimd
        def _(pool):
            def rsqrt(out, in_, ready, n, done):
                pool.wait_ge(ready, n + 1)
                nc.gpsimd.tensor_tensor(out[:, :], in_[:, :], power[:, :], ALU.pow).then_inc(done, 1)

            def model_norm(n, p):
                wait(pool, res_normed, 2 * (n - 1))
                rsqrt(rstd0[p], var0, ln0_var, 2 * n + 1, ln0_rstd)

            def layer_norm(n):
                wait(pool, ln_done, n)
                rsqrt(rstd, var, ln_var, n, ln_rstd)
                pool.wait_ge(ln_rstd, n + 1)
                pool.wait_ge(ln_mom, 6 * n + 6)
                nc.gpsimd.tensor_tensor(shift[:, :], mom[:, 5, :], rstd[:, :], ALU.mult).then_inc(ln_shift, 1)

            def second_operands(n):
                pool.wait_ge(dops, 2 * n + 2)
                wait(pool, ec_ready, NB * n)
                nc.gpsimd.tensor_tensor(dmov[:, 1, :, :], dmovT[:, 1, :].unsqueeze(1).broadcast_to([P, NH, P]), mask[:, :, :],
                                        ALU.mult).then_inc(dmov2_done, 1)

            def add_squares(n, t):
                pool.wait_ge(y_sq, T * n + t + 1)
                wait(pool, sq_added, (T - 1) * n + t - 1)
                nc.gpsimd.tensor_tensor(sq[:, 0, :], sq[:, 0, :], sq[:, t, :], ALU.add).then_inc(sq_added, 1)

            def norm_residual(n, c, p):
                pool.wait_ge(res_in[p], 16 * (c + 1))
                pool.wait_ge(ln0_rstd, n + 1)
                nc.gpsimd.tensor_tensor(hres[p][:, :, :], hres[p][:, :, :], mean0[p][:, :].unsqueeze(2).broadcast_to([P, NB, DM]),
                                        ALU.subtract).then_inc(res_normed, 1)
                pool.wait_ge(res_normed, 2 * n + 1)
                nc.gpsimd.tensor_tensor(hres[p][:, :, :], hres[p][:, :, :], rstd0[p][:, :].unsqueeze(2).broadcast_to([P, NB, DM]),
                                        ALU.mult).then_inc(res_normed, 1)

            def gate(n, t):
                pool.wait_ge(y_skip, T * n + t + 1)
                pool.wait_ge(z_done, T * n + T)
                nc.gpsimd.tensor_tensor(yg[:, t, :], yg[:, t, :], sz[:, t, :], ALU.mult).then_inc(y_gated, 1)

            def first_tap(n, layer, p, i):
                q = QORDER[i]
                pool.wait_ge(x_raw, QCONV * n + i + 1)
                if i == 0:
                    pool.wait_ge(halo_set, n + 1)
                    wait(pool, y_skip, T * (n - 1))
                nc.gpsimd.tensor_tensor(xc[p][:, q, :].rearrange("p (b i) -> p b i", b=NB), xpad[:, q, :, 0:P],
                                        vector(layer, "conv_w", q * TAPS, 1).unsqueeze(2).broadcast_to([P, NB, P]), ALU.mult).then_inc(tap0, 1)

            def to_end(n, p, b):
                pool.wait_ge(dtx_done, NB * n + b + 1)
                if b == 0:
                    pool.wait_ge(decay_done, 3 * n + 3)
                    wait(pool, st_ready, 2 * n)
                nc.gpsimd.tensor_tensor(wx[:, b, :, :], dtx[:, b, :, :], decay[p][:, b, :].unsqueeze(2).broadcast_to([P, NH, HD]),
                                        ALU.mult).then_inc(wx_done, 1)

            def decay_state(n, p):
                wait(pool, state_done, 2 * n)
                if isinstance(n, int) and n < GROUPS:
                    pool.wait_ge(cleared, 1)
                nc.gpsimd.tensor_tensor(sdec[:, :, :, :], state[p][:, :, :, :], sdecay[p][:, :, :].unsqueeze(3).broadcast_to([P, NB, T, HD]),
                                        ALU.mult).then_inc(sdec_done, 1)

            def step(n, layer, c, p):
                more, next_layer = follows(n, 1), layer_of(n, layer, 1)
                twice = layer_of(n, layer, 2) == 0
                if more:
                    first_tap(n + 1, next_layer, 1 - p, 0)
                to_end(n, p, 0)
                if follows(n, 2):
                    layer_norm(n + 2)
                to_end(n, p, 1)
                if more:
                    first_tap(n + 1, next_layer, 1 - p, 1)
                to_end(n, p, 2)
                if more:
                    first_tap(n + 1, next_layer, 1 - p, 2)
                to_end(n, p, 3)
                decay_state(n, p)
                if twice:
                    model_norm(n + 2, p)
                if next_layer == 0:
                    norm_residual(n + 1, c + p, 1 - p)
                if more:
                    first_tap(n + 1, next_layer, 1 - p, 3)
                    first_tap(n + 1, next_layer, 1 - p, 4)
                gate(n, 0)
                gate(n, 1)
                for t in range(2, T):
                    gate(n, t)
                    add_squares(n, t - 1)
                add_squares(n, T - 1)
                if follows(n, 1):
                    second_operands(n + 1)
                rsqrt(rrms, ssq, ss_done, n, rr_done)

            for g in range(GROUPS):
                nc.gpsimd.memset(halo[g][:, :, :, :], 0.0)
            pool.wait_ge(ones_ready, 1)
            layer_norm(0)
            model_norm(0, 0)
            for g in range(GROUPS):
                last = nc.gpsimd.memset(state[g][:, :, :, :], 0.0)
            last.then_inc(cleared, 1)
            layer_norm(1)
            model_norm(1, 1)
            for i in range(QCONV):
                first_tap(0, 0, 0, i)
            pool.wait_ge(consts_ready, 3)
            second_operands(0)
            norm_residual(0, 0, 0)
            over_items(pool, step)

        @block.vector
        def _(dve):
            def layer_moments(n, layer, c, p):
                dve.wait_ge(h_in[p], 16 * (CHUNKS * layer + c + 1))
                wait(dve, ln_shift, n)
                twice = dict(factor=1.0 + EPS, eps=EPS * EPS) if layer == 0 else {}
                moments(nc, dve, [hin[p][:, b, :] for b in range(NB)], stats, mom, var[:, :], ln_stats, ln_mom, ln_var, n, sign=-1, **twice)
                if layer == 0:
                    wait(dve, ln0_rstd, n)
                    wait(dve, res_normed, 2 * (n - 1))
                    nc.vector.tensor_scalar(mean0[p][:, :], mom[:, 0, :], 0.5, None, ALU.mult).then_inc(ln0_var, 1)
                    nc.vector.tensor_scalar(var0[:, :], mom[:, 4, :], 1.0 / DM, EPS, ALU.mult, ALU.add).then_inc(ln0_var, 1)

            def fold_rows(layer):
                dve.wait_ge(vec_in, 16)
                wait(dve, bias_summed, layer)
                for kd in range(KD):
                    nc.vector.tensor_scalar(lnb_rows[:, kd, :], ones[:, :], vector(layer, "ln_b", kd, 1), None, ALU.mult).then_inc(rows_ready, 1)

            def fold_weights(layer):
                for kd in range(KD):
                    dve.wait_ge(hi_ready, KD * layer + kd + 1)
                    nc.vector.scalar_tensor_tensor(wlo[:, kd, :], raw[:, kd, :], vector(layer, "ln_w", kd, 1), whi[:, kd, :].bitcast(F32),
                                                   ALU.mult, ALU.subtract).then_inc(lo_ready, 1)

            def keep_bias(layer):
                dve.wait_ge(bias_summed, layer + 1)
                nc.vector.tensor_copy(pbias[:, layer, :], ybank[1][:, BIAS_AT:BIAS_AT + 2 * T + 1])
                at = BIAS_AT + 2 * T + 1
                nc.vector.tensor_tensor(dtb[:, layer, :], ybank[1][:, at:at + NH], vector(layer, "dt_bias"), ALU.add).then_inc(bias_ready, 1)

            def fold_outputs(layer):
                dve.wait_ge(wo_in, 16 * LAYERS)
                for t in range(T):
                    last = nc.vector.tensor_scalar(wo[layer][:, t, :], wo[layer][:, t, :], vector(layer, "rms_w", t, 1), None, ALU.mult)
                last.then_inc(wo_ready, 1)

            def round_constants():
                dve.wait_ge(consts_in, 32)
                nc.vector.tensor_copy(identb[:, :], ident[:, :]).then_inc(consts_ready, 1)
                nc.vector.tensor_copy(mask[:, :, :], staged[:, 0:NH * P].rearrange("p (h i) -> p h i", h=NH)).then_inc(consts_ready, 1)
                nc.vector.tensor_copy(sel[:, :, :], staged[:, NH * P:NH * P + 2 * P].rearrange("p (o m) -> p o m", o=2)).then_inc(consts_ready, 1)

            def rest_u(n):
                for kd in range(KD):
                    dve.wait_ge(u_hi, KD * n + kd + 1)
                    nc.vector.tensor_tensor(ulo[:, kd, :], front[kd][:, :], uhi[:, kd, :].bitcast(F32), ALU.subtract).then_inc(u_lo, 1)

            def bias_dt(n, layer):
                if starts_layer(n):
                    dve.wait_ge(bias_ready, layer + 1)
                dve.wait_ge(dt_turned, n + 1)
                nc.vector.tensor_tensor(dtraw[:, :, :], front[0][:, :].rearrange("p (b h) -> p b h", b=NB)[:, :, 0:NH],
                                        dtb[:, layer, :].unsqueeze(1).broadcast_to([P, NB, NH]), ALU.add).then_inc(dt_biased, 1)

            def finish_dt(n, layer, p):
                dve.wait_ge(dt_ln, n + 1)
                nc.vector.scalar_tensor_tensor(dtv[p][:, :, :], dtraw[:, :, :], 0.0, dtln[:, :, :], ALU.max, ALU.add).then_inc(dt_done, 1)
                dve.wait_ge(dt_done, n + 1)
                nc.vector.tensor_tensor(da[:, :, :], dtv[p][:, :, :], aneg[:, layer, :].unsqueeze(1).broadcast_to([P, NB, NH]),
                                        ALU.mult).then_inc(da_done, 1)

            def split_sums(n):
                dve.wait_ge(da_summed, n + 1)
                wait(dve, decay_done, 3 * n)
                nc.vector.tensor_copy(sums[:, :, :, :].rearrange("p s b h -> p (s b h)"), front[0][:, 0:3 * NB * NH]).then_inc(sums_out, 1)
                wait(dve, cum_turned, n)

                def part(i, of):
                    to = cum3[:, :, 0:2 * PARTS * NH].rearrange("p b (d i h) -> p b d i h", d=2, i=PARTS)[:, :, :, i, :]
                    return nc.vector.tensor_copy(to, of.unsqueeze(2).broadcast_to([P, NB, 2, NH])).then_inc(split, 1)

                def rest(out, of, i):
                    return nc.vector.tensor_tensor(out[:, :, :], of, cum3[:, :, i * NH:(i + 1) * NH], ALU.subtract).then_inc(split, 1)

                cum = sums[:, 0, :, :]
                dve.wait_ge(sums_out, n + 1)
                part(0, cum)
                dve.wait_ge(split, 5 * n + 1)
                rest(rest1, cum, 0)
                dve.wait_ge(split, 5 * n + 2)
                part(1, rest1[:, :, :])
                dve.wait_ge(split, 5 * n + 3)
                rest(rest2, rest1[:, :, :], 1)
                dve.wait_ge(split, 5 * n + 4)
                part(2, rest2[:, :, :])

            def decay_operands(n):
                dve.wait_ge(cum_turned, n + 1)
                wait(dve, dmov2_done, n)
                turned = front[1][:, 0:P].bitcast(BF16)
                for i, to in enumerate((dstat, dmovT)):
                    nc.vector.tensor_scalar(to[:, :, :].rearrange("p a j -> p (a j)"), turned, col[:, 2 * i:2 * i + 1], col[:, 2 * i + 1:2 * i + 2],
                                            ALU.mult, ALU.add).then_inc(dops, 1)
                dve.wait_ge(dops, 2 * n + 2)
                wait(dve, ec_ready, NB * n)
                nc.vector.tensor_tensor(dmov[:, 0, :, :], dmovT[:, 0, :].unsqueeze(1).broadcast_to([P, NH, P]), mask[:, :, :],
                                        ALU.mult).then_inc(dmov_done, 1)

            def set_halo(n, g):
                wait(dve, taps, 3 * QCONV * n)
                wait(dve, halo_kept, n)
                if isinstance(n, int) and n < GROUPS:
                    dve.wait_ge(cleared, 1)
                nc.vector.tensor_copy(xpad[:, :, :, 0:HALO].rearrange("p q b i -> p (q b) i"),
                                      halo[g][:, :, :, :].rearrange("p q b i -> p (q b) i")).then_inc(halo_set, 1)

            def keep_halo(n, g):
                dve.wait_ge(x_raw, QCONV * n + QCONV)
                nc.vector.tensor_copy(halo[g][:, :, :, :].rearrange("p q b i -> p (q b) i"),
                                      xpad[:, :, :, P:P + HALO].rearrange("p q b i -> p (q b) i")).then_inc(halo_kept, 1)

            def clear_halo(n, g):
                dve.wait_ge(halo_kept, n + 1)
                nc.vector.memset(halo[g][:, :, :, :], 0.0).then_inc(halo_cleared, 1)
                dve.wait_ge(halo_cleared, n // ITEMS * GROUPS + g + 1)

            def convolve(n, layer, p, i):
                q = QORDER[i]
                to = xc[p][:, q, :].rearrange("p (b i) -> p b i", b=NB)
                dve.wait_ge(tap0, QCONV * n + i + 1)
                for tap in range(1, TAPS):
                    if tap > 1:
                        dve.wait_ge(taps, 3 * QCONV * n + 3 * i + tap - 1)
                    nc.vector.scalar_tensor_tensor(to, xpad[:, q, :, tap:tap + P], vector(layer, "conv_w", q * TAPS + tap, 1), to, ALU.mult, ALU.add).then_inc(taps, 1)

            def mask_scores(n):
                dve.wait_ge(g_done, n + 1)
                nc.vector.tensor_tensor(gm[:, :, :], ybank[0][:, :].rearrange("p (b i) -> p b i", b=NB),
                                        tri[:, :].unsqueeze(1).broadcast_to([P, NB, P]), ALU.mult).then_inc(gm_done, 1)

            def weigh(n, q):
                b, half = q // 2, q % 2
                dve.wait_ge(d_exp, 8 * n + q + 1)
                if q == 0:
                    dve.wait_ge(gm_done, n + 1)
                nc.vector.tensor_tensor(m[:, b, 4 * half:4 * half + 4, :], expd[:, half, :, :],
                                        gm[:, b, :].unsqueeze(1).broadcast_to([P, NH // 2, P]), ALU.mult).then_inc(m_done, 1)

            def scale_x(n, p, b):
                dve.wait_ge(xt_done, NB * n + b + 1)
                nc.vector.tensor_tensor(dtx[:, b, :, :], mix[(b + 1) % 2][:, :].rearrange("p (h d) -> p h d", h=NH),
                                        dtv[p][:, b, :].unsqueeze(2).broadcast_to([P, NH, HD]), ALU.mult).then_inc(dtx_done, 1)

            def scale_c(n, b):
                dve.wait_ge(ec_exp, NB * n + b + 1)
                nc.vector.tensor_tensor(cs[:, b, :, :], ecum[:, b % 2, :, :], cc[:, b * P:(b + 1) * P].unsqueeze(1).broadcast_to([P, T, P]),
                                        ALU.mult).then_inc(cs_done, 1)

            def skip(n, layer, p, t):
                dve.wait_ge(y_ready, T * n + t + 1)
                nc.vector.scalar_tensor_tensor(yg[:, t, :], xc[p][:, t, :], vector(layer, "D", t, 1), ybank[t % 2][:, :], ALU.mult, ALU.add).then_inc(y_skip, 1)

            def add_state(n, p):
                dve.wait_ge(sdec_done, n + 1)
                if ends_sequence(n):
                    for s in range(2):
                        dve.wait_ge(st_ready, 2 * n + s + 1)
                        nc.vector.memset(state[p][:, 2 * s:2 * s + 2, :, :], 0.0).then_inc(state_done, 1)
                    return
                for s in range(2):
                    dve.wait_ge(st_ready, 2 * n + s + 1)
                    nc.vector.tensor_tensor(state[p][:, 2 * s:2 * s + 2, :, :], mix[s][:, :].rearrange("p (b t d) -> p b t d", b=2, t=T),
                                            sdec[:, 2 * s:2 * s + 2, :, :], ALU.add).then_inc(state_done, 1)

            def mean_square(n):
                dve.wait_ge(ss_ready, n + 1)
                nc.vector.tensor_scalar(ssq[:, :], ybank[1][:, 0:NB], 1.0 / DI, EPS, ALU.mult, ALU.add).then_inc(ss_done, 1)

            def finish(n, layer, c, p, s):
                if s == 0:
                    dve.wait_ge(rr_done, n + 1)
                    if layer == 0:
                        dve.wait_ge(res_normed, 2 * n + 2)
                    else:
                        dve.wait_ge(res_in[p], 16 * (CHUNKS * layer + c + 1))
                dve.wait_ge(o_ready, 2 * n + s + 1)
                for b in (2 * s, 2 * s + 1):
                    nc.vector.scalar_tensor_tensor(hres[p][:, b, :], mix[1 - s][:, (b % 2) * DM:(b % 2 + 1) * DM], rrms[:, b:b + 1],
                                                   hres[p][:, b, :], ALU.mult, ALU.add).then_inc(h_done, 1)

            def front_part(n, p):
                fold_weights(0)
                rest_u(n)
                round_constants()
                layer_moments(n + 1, 0, 0, 1 - p)
                keep_bias(0)
                set_halo(n, p)
                bias_dt(n, 0)
                finish_dt(n, 0, p)
                convolve(n, 0, p, 0)
                for i in range(1, QCONV):
                    convolve(n, 0, p, i)
                    if i == 1:
                        split_sums(n)
                    if i == 2:
                        decay_operands(n)
                keep_halo(n, p)
                start_scan(n)
                rest_u(n + 1)
                weigh(n, 1)
                weigh(n, 2)
                for i in range(LAYERS):
                    fold_outputs(i)

            def start_scan(n):
                mask_scores(n)
                weigh(n, 0)

            def step(n, layer, c, p):
                more, more2 = follows(n, 1), follows(n, 2)
                layer1, layer2 = layer_of(n, layer, 1), layer_of(n, layer, 2)
                chunk2 = 0 if ends_sequence(n) else c + 1
                if more:
                    set_halo(n + 1, 1 - p)
                    bias_dt(n + 1, layer1)
                weigh(n, 3)
                if more2:
                    layer_moments(n + 2, layer2, chunk2, p)
                scale_x(n, p, 0)
                weigh(n, 4)
                if follows_any(n):
                    finish(n - 1, layer_of(n, layer, -1), None, 1 - p, 1)
                scale_x(n, p, 1)
                weigh(n, 5)
                scale_x(n, p, 2)
                scale_x(n, p, 3)
                if more:
                    convolve(n + 1, layer1, 1 - p, 0)
                weigh(n, 6)
                weigh(n, 7)
                for b in range(NB):
                    scale_c(n, b)
                if more:
                    convolve(n + 1, layer1, 1 - p, 1)
                    finish_dt(n + 1, layer1, 1 - p)
                skip(n, layer, p, 0)
                if more:
                    split_sums(n + 1)
                skip(n, layer, p, 1)
                if more:
                    decay_operands(n + 1)
                    convolve(n + 1, layer1, 1 - p, 2)
                skip(n, layer, p, 2)
                if more:
                    convolve(n + 1, layer1, 1 - p, 3)
                skip(n, layer, p, 3)
                if more:
                    convolve(n + 1, layer1, 1 - p, 4)
                add_state(n, p)
                if ends_sequence(n) and more2:
                    clear_halo(n, p)
                if more:
                    keep_halo(n + 1, 1 - p)
                    mask_scores(n + 1)
                    weigh(n + 1, 0)
                if more2:
                    if starts_layer(n + 2):
                        fold_rows(layer2)
                    rest_u(n + 2)
                    if starts_layer(n + 2):
                        fold_weights(layer2)
                mean_square(n)
                if more:
                    weigh(n + 1, 1)
                finish(n, layer, c, p, 0)
                if more:
                    weigh(n + 1, 2)
                if starts_layer(n + 2):
                    keep_bias(layer2)

            nc.vector.memset(ones[:, :], 1.0)
            nc.vector.memset(power[:, :], -0.5).then_inc(ones_ready, 1)
            nc.vector.memset(dtT[:, :], 0.0)
            nc.vector.memset(cum3[:, :, :], 0.0).then_inc(ones_ready, 1)
            dve.wait_ge(ones_ready, 2)
            layer_moments(0, 0, 0, 0)
            fold_rows(0)
            dve.wait_ge(aexp_ready, 1)
            nc.vector.tensor_scalar(aneg[:, :, :], aexp[:, :, :], -1.0, None, ALU.mult)
            front_part(0, 0)
            over_items(dve, step)
            finish(LAYERS * ITEMS - 1, LAYERS - 1, None, 1, 1)


def mlp(nc, h, x, out, w):
    with ExitStack() as keep:
        def sb(name, shape, dt=F32):
            return keep.enter_context(nc.sbuf_tensor(f"M_{name}", shape, dt))

        whi = sb("whi", [P, 2 * BLOCKS, KD, DM], F32R)
        wlo = sb("wlo", [P, 2 * BLOCKS, KD, DM], F32R)
        ident = sb("ident", [P, P])
        rowsel = sb("rowsel", [PARTS * 32, P], BF16)
        bias3 = sb("bias3", [PARTS * 32, BLOCKS, DM], BF16)
        bias = sb("bias", [P, BLOCKS, KD])
        gamma = sb("gamma", [P, BLOCKS, KD])
        beta = sb("beta", [P, BLOCKS, KD])
        power = sb("power", [P, NB])
        hin, xin = ([sb(f"{name}{s}", [P, NB, DM]) for s in range(2)] for name in ("hin", "xin"))
        h_in = [nc.alloc_semaphore(name=f"M_h_in{s}") for s in range(2)]

        def load(sp, i, s):
            for to, of in ((hin, h), (xin, x)):
                sp.dma_start(to[s][:, :, :], item_tokens(of, i, s)).then_inc(h_in[s], 16)

        prepare_mlp(nc, w, locals())
        mlp_items(nc, out, locals())


def prepare_mlp(nc, w, k):
    whi, wlo, ident, rowsel, bias3, bias, gamma, beta, power = (
        k[n] for n in ("whi", "wlo", "ident", "rowsel", "bias3", "bias", "gamma", "beta", "power"))
    load = k["load"]
    N = 2 * BLOCKS
    with ExitStack() as ctx:
        def sb(name, shape, dt=F32):
            return ctx.enter_context(nc.sbuf_tensor(f"M_{name}", shape, dt))

        def sem(name):
            return nc.alloc_semaphore(name=f"M_{name}")

        q = sb("q", [P, N, KD, DM], I32)
        steps = sb("steps", [P, N, KD, DM])
        scaled = sb("scaled", [P, 2, KD, DM])
        full = sb("full", [P, N, KD, DM])
        scales = sb("scales", [DM // QGROUP, N, DM])
        spread = sb("spread", [DM // QGROUP, DM])
        la = sb("la", [RANK, N, DM])
        lb = sb("lb", [RANK, N, DM])
        brow = sb("brow", [P, BLOCKS, DM])
        part = [sb(f"part{i}", [P, BLOCKS, DM], BF16) for i in range(PARTS)]
        rest = [sb(f"rest{i}", [P, BLOCKS, DM]) for i in range(PARTS - 1)]
        rowself = sb("rowself", [PARTS * 32, P])
        scale_ps = [ctx.enter_context(nc.psum_tensor(f"M_scale_ps{i}", [P, KD, DM], F32)) for i in range(2)]
        lora_ps = [ctx.enter_context(nc.psum_tensor(f"M_lora_ps{i}", [P, KD, DM], F32)) for i in range(2)]
        loaded, spreadout, stepped, scaled_done, full_done, hi_done, lo_done = (
            sem(x) for x in ("loaded", "spreadout", "stepped", "scaled_done", "full_done", "hi_done", "lo_done"))
        split, prepared = sem("split"), sem("prepared")
        block = ctx.enter_context(nc.Block())

        loads = [
            (q[:, :, :, :], w["qweights"].rearrange("j (k p) o -> p j k o", p=P)),
            (scales[:, :, :], w["scales"].rearrange("j g o -> g j o")),
            (spread[:, :], w["spread"]),
            (la[:, :, :], w["lora_a"].rearrange("j r d -> r j d")),
            (lb[:, :, :], w["lora_b"].rearrange("j r o -> r j o")),
            (brow[:, :, :], w["biases"].rearrange("(m e) o -> e m o", e=2)[0].partition_broadcast(P)),
            (ident[:, :], w["constants"][:, C_IDENT:C_IDENT + P]),
            (rowself[:, :], w["rowsel"]),
            (gamma[:, :, :], w["gamma"].rearrange("m p k -> p m k")),
            (beta[:, :, :], w["beta"].rearrange("m p k -> p m k")),
        ]
        for m in range(BLOCKS):
            loads.append((bias[:, m, :], w["bias_columns"][2 * m + 1]))
        LOADED = 16 * len(loads)

        @block.sync
        def _(sp):
            for to, of in loads[0::2]:
                sp.dma_start(to, of).then_inc(loaded, 16)
            for s in range(2):
                load(sp, 0, s)

        @block.scalar
        def _(act):
            for to, of in loads[1::2]:
                act.dma_start(to, of).then_inc(loaded, 16)
            for j in range(N):
                act.wait_ge(full_done, j + 1)
                nc.scalar.activation(whi[:, j, :, :], full[:, j, :, :], ACT.Copy).then_inc(hi_done, 1)

        @block.tensor
        def _(pe):
            pe.wait_ge(loaded, LOADED)
            for j in range(N):
                wait(pe, full_done, j - 1)
                for kd in range(KD):
                    nc.tensor.matmul(scale_ps[j % 2][:, kd, :], spread[:, kd * P:(kd + 1) * P], scales[:, j, :], start=True, stop=True)
                    last = nc.tensor.matmul(lora_ps[j % 2][:, kd, :], la[:, j, kd * P:(kd + 1) * P], lb[:, j, :], start=True, stop=True)
                last.then_inc(spreadout, 1)

        @block.vector
        def _(dve):
            def low_part(j):
                dve.wait_ge(hi_done, j + 1)
                nc.vector.tensor_tensor(wlo[:, j, :, :], full[:, j, :, :], whi[:, j, :, :].bitcast(F32), ALU.subtract).then_inc(lo_done, 1)

            nc.vector.memset(power[:, :], -0.5)
            dve.wait_ge(loaded, LOADED)
            nc.vector.tensor_scalar(steps[:, :, :, :], q[:, :, :, :], 1.0 / 7.5, -1.0, ALU.mult, ALU.add).then_inc(stepped, 1)
            dve.wait_ge(stepped, 1)
            left = brow
            for i in range(PARTS):
                nc.vector.tensor_copy(part[i][:, :, :], left[:, :, :]).then_inc(split, 1)
                dve.wait_ge(split, 2 * i + 1)
                nc.vector.tensor_copy(bias3[32 * i:32 * i + 32, :, :], part[i][32 * i:32 * i + 32, :, :])
                if i < PARTS - 1:
                    nc.vector.tensor_tensor(rest[i][:, :, :], left[:, :, :], part[i][:, :, :], ALU.subtract).then_inc(split, 1)
                    dve.wait_ge(split, 2 * i + 2)
                    left = rest[i]
            nc.vector.tensor_copy(rowsel[:, :], rowself[:, :]).then_inc(prepared, 1)
            dve.wait_ge(prepared, 1)
            for j in range(N):
                dve.wait_ge(spreadout, j + 1)
                nc.vector.tensor_tensor(scaled[:, j % 2, :, :], steps[:, j, :, :], scale_ps[j % 2][:, :, :], ALU.mult).then_inc(scaled_done, 1)
                dve.wait_ge(scaled_done, j + 1)
                nc.vector.tensor_tensor(full[:, j, :, :], scaled[:, j % 2, :, :], lora_ps[j % 2][:, :, :], ALU.add).then_inc(full_done, 1)
                if j > 0:
                    low_part(j - 1)
            low_part(N - 1)
            dve.wait_ge(lo_done, N)


def mlp_items(nc, out, k):
    whi, wlo, ident, rowsel, bias3, bias, gamma, beta, power = (
        k[n] for n in ("whi", "wlo", "ident", "rowsel", "bias3", "bias", "gamma", "beta", "power"))
    hin, xin, h_in, load = (k[n] for n in ("hin", "xin", "h_in", "load"))
    with ExitStack() as ctx:
        def sb(name, shape, dt=F32):
            return [ctx.enter_context(nc.sbuf_tensor(f"M_{name}{s}", shape, dt)) for s in range(2)]

        def sem(name):
            return nc.alloc_semaphore(name=f"M_{name}")

        x1, normed = (sb(n, [P, NB, DM]) for n in ("x1", "normed"))
        nrm, outb = sb("nrm", [P, NB, DM]), sb("outb", [P, NB, DM])
        hT, g = sb("hT", [P, KD, W]), sb("g", [P, KD, W])
        hhi, hlo = sb("hhi", [P, KD, W], F32R), sb("hlo", [P, KD, W], F32R)
        ghi, glo = sb("ghi", [P, KD, W], F32R), sb("glo", [P, KD, W], F32R)
        stats, var, rstd, shift = (sb(n, [P, NB, c]) for n, c in (("stats", 6), ("var", 1), ("rstd", 1), ("shift", 1)))
        stats0, var0, rstd0 = (sb(n, [P, NB, c]) for n, c in (("stats0_", 6), ("var0_", 1), ("rstd0_", 1)))
        mom, mom0 = sb("mom", [P, 6, NB]), sb("mom0_", [P, 6, NB])
        lin = [[ctx.enter_context(nc.psum_tensor(f"M_lin{s}{i}", [P, 512], F32)) for i in range(2)] for s in range(2)]
        turn = [[ctx.enter_context(nc.psum_tensor(f"M_turn{s}{i}", [P, 512], F32)) for i in range(2)] for s in range(2)]

        x1_done, n0_stats, n0_mom, n0_var, n0_rstd, n0_done = (sem(n) for n in ("x1_done", "n0_stats", "n0_mom", "n0_var", "n0_rstd", "n0_done"))
        in_turned, in_copied = sem("in_turned"), sem("in_copied")
        h_hi, h_lo = sem("h_hi"), sem("h_lo")
        first_done = sem("first_done")
        b_stats, b_mom, b_var, b_rstd, b_shift = (sem(n) for n in ("b_stats", "b_mom", "b_var", "b_rstd", "b_shift"))
        b_normed = sem("b_normed")
        b_turned, b_gelu, g_hi, g_lo = (sem(n) for n in ("b_turned", "b_gelu", "g_hi", "g_lo"))
        second_done, h_added = sem("second_done"), sem("h_added")
        x_saved = sem("x_saved")
        out_turned, out_added = sem("out_turned"), sem("out_added")
        stored = [sem(f"stored{s}") for s in range(2)]
        PAIRS = ITEMS // 2

        def turn_of(i, s, m):
            return 2 * BLOCKS * i + 2 * m + s

        def follows_pair(i):
            return not isinstance(i, int) or i + 1 < PAIRS

        def precedes_pair(i):
            return not isinstance(i, int) or i > 0

        def over_pairs(eng, step):
            step(0)
            with eng.Fori(1, PAIRS - 1) as i:
                step(i)
            step(PAIRS - 1)

        block = ctx.enter_context(nc.Block())

        @block.sync
        def _(sp):
            def load_next(i, s):
                wait(sp, x_saved, 2 * (i - 1) + s + 1)
                load(sp, i, s)

            def store(i, s):
                sp.wait_ge(out_added, 2 * (2 * i + s) + 2)
                sp.dma_start(item_tokens(out, i, s), outb[s][:, :, :]).then_inc(stored[s], 16)

            def step(i):
                if follows_pair(i):
                    load_next(i + 1, 0)
                if precedes_pair(i):
                    store(i - 1, 1)
                if follows_pair(i):
                    load_next(i + 1, 1)
                store(i, 0)

            over_pairs(sp, step)
            store(PAIRS - 1, 1)
            for s in range(2):
                sp.wait_ge(stored[s], 16 * PAIRS)

        @block.tensor
        def _(pe):
            def turn_in(i, s):
                n = 2 * i + s
                pe.wait_ge(n0_done, n + 1)
                wait(pe, b_gelu, 2 * (turn_of(i, s, 0) - 1))
                for kd in range(KD):
                    for b in range(NB):
                        last = nc.tensor.transpose(turn[s][kd][:, b * P:(b + 1) * P], normed[s][:, b, kd * P:(kd + 1) * P], ident[:, :])
                    last.then_inc(in_turned, 1)

            def first_linear(i, s, m):
                n = turn_of(i, s, m)
                pe.wait_ge(h_lo, 2 * n + 2)
                if m == 0:
                    wait(pe, out_added, 2 * (2 * i + s - 1))
                for b in range(NB):
                    to = lin[s][b // 2][:, (b % 2) * DM:(b % 2 + 1) * DM]
                    nc.tensor.matmul(to, rowsel[:, :], bias3[:, m, :], start=True, stop=False, skip_group_check=True)
                    passes = [(kd, a, ww) for kd in range(KD) for a, ww in ((hhi, whi), (hhi, wlo), (hlo, whi))]
                    for j, (kd, a, ww) in enumerate(passes):
                        last = nc.tensor.matmul(to, a[s][:, kd, b * P:(b + 1) * P], ww[:, 2 * m, kd, :],
                                                start=False, stop=j == len(passes) - 1, skip_group_check=True)
                    if b % 2:
                        last.then_inc(first_done, 1)

            def turn_normed(i, s, m):
                n = turn_of(i, s, m)
                for b in range(NB):
                    pe.wait_ge(b_normed, NB * n + b + 1)
                    for kd in range(KD):
                        last = nc.tensor.transpose(turn[s][kd][:, b * P:(b + 1) * P], nrm[s][:, b, kd * P:(kd + 1) * P], ident[:, :])
                        if b == NB - 1:
                            last.then_inc(b_turned, 1)

            def second_linear(i, s, m):
                n = turn_of(i, s, m)
                pe.wait_ge(g_lo, 2 * n + 2)
                for o in range(KD):
                    passes = [(kd, ww, a) for kd in range(KD) for ww, a in ((whi, ghi), (wlo, ghi), (whi, glo))]
                    for j, (kd, ww, a) in enumerate(passes):
                        last = nc.tensor.matmul(lin[s][o][:, :], ww[:, 2 * m + 1, kd, o * P:(o + 1) * P], a[s][:, kd, :],
                                                start=j == 0, stop=j == len(passes) - 1)
                    last.then_inc(second_done, 1)

            def turn_out(i, s):
                n = turn_of(i, s, BLOCKS - 1)
                pe.wait_ge(h_added, 2 * n + 2)
                for b in range(NB):
                    for kd in range(KD):
                        last = nc.tensor.transpose(lin[s][b // 2][:, (b % 2) * DM + kd * P:(b % 2) * DM + (kd + 1) * P],
                                                   hT[s][:, kd, b * P:(b + 1) * P], ident[:, :])
                    if b % 2:
                        last.then_inc(out_turned, 1)

            def step(i):
                for m in range(BLOCKS):
                    first_linear(i, 0, m)
                    if m > 0:
                        second_linear(i, 1, m - 1)
                    else:
                        if precedes_pair(i):
                            second_linear(i - 1, 1, BLOCKS - 1)
                        turn_in(i, 1)
                        if precedes_pair(i):
                            turn_out(i - 1, 1)
                    turn_normed(i, 0, m)
                    first_linear(i, 1, m)
                    second_linear(i, 0, m)
                    if m == BLOCKS - 1:
                        if follows_pair(i):
                            turn_in(i + 1, 0)
                        turn_out(i, 0)
                    turn_normed(i, 1, m)

            turn_in(0, 0)
            over_pairs(pe, step)
            second_linear(PAIRS - 1, 1, BLOCKS - 1)
            turn_out(PAIRS - 1, 1)

        @block.scalar
        def _(act):
            def copy_in(i, s):
                n = 2 * i + s
                wait(act, out_turned, 2 * (n - 1))
                for kd in range(KD):
                    act.wait_ge(in_turned, 2 * n + kd + 1)
                    nc.scalar.activation(hT[s][:, kd, :], turn[s][kd][:, :], ACT.Copy).then_inc(in_copied, 1)

            def normalise(i, s, m):
                n = turn_of(i, s, m)
                act.wait_ge(b_shift, n + 1)
                for b in range(NB):
                    nc.scalar.activation(nrm[s][:, b, :], lin[s][b // 2][:, (b % 2) * DM:(b % 2 + 1) * DM], ACT.Identity,
                                         bias=shift[s][:, b, :], scale=rstd[s][:, b, :]).then_inc(b_normed, 1)

            def gelu(i, s, m):
                n = turn_of(i, s, m)
                for kd in range(KD):
                    act.wait_ge(b_turned, 2 * n + kd + 1)
                    nc.scalar.activation(g[s][:, kd, :], turn[s][kd][:, :], ACT.Gelu,
                                         bias=beta[:, m, kd:kd + 1], scale=gamma[:, m, kd:kd + 1]).then_inc(b_gelu, 1)
                for kd in range(KD):
                    act.wait_ge(b_gelu, 2 * n + kd + 1)
                    nc.scalar.activation(ghi[s][:, kd, :], g[s][:, kd, :], ACT.Copy).then_inc(g_hi, 1)

            def save_x(i, s):
                n = 2 * i + s
                act.wait_ge(x1_done, n + 1)
                wait(act, out_added, 2 * (n - 1))
                nc.scalar.activation(x1[s][:, :, :], hin[s][:, :, :], ACT.Copy).then_inc(x_saved, 1)

            def step(i):
                for m in range(BLOCKS):
                    normalise(i, 0, m)
                    if m == 0:
                        copy_in(i, 1)
                    gelu(i, 0, m)
                    if m == 0:
                        save_x(i, 1)
                    normalise(i, 1, m)
                    if m == BLOCKS - 1 and follows_pair(i):
                        copy_in(i + 1, 0)
                    gelu(i, 1, m)
                if follows_pair(i):
                    save_x(i + 1, 0)

            copy_in(0, 0)
            save_x(0, 0)
            over_pairs(act, step)

        @block.gpsimd
        def _(pool):
            def rsqrt(out, in_, ready, n, done):
                pool.wait_ge(ready, n + 1)
                nc.gpsimd.tensor_tensor(out[:, :, 0], in_[:, :, 0], power[:, :], ALU.pow).then_inc(done, 1)

            def block_scale(i, s, m):
                n = turn_of(i, s, m)
                rsqrt(rstd[s], var[s], b_var, n, b_rstd)
                pool.wait_ge(b_rstd, n + 1)
                pool.wait_ge(b_mom, 6 * n + 6)
                nc.gpsimd.tensor_tensor(shift[s][:, :, 0], mom[s][:, 5, :], rstd[s][:, :, 0], ALU.mult).then_inc(b_shift, 1)

            def step(i):
                for m in range(BLOCKS):
                    for s in range(2):
                        block_scale(i, s, m)
                    if m + 1 < BLOCKS and follows_pair(i):
                        rsqrt(rstd0[m], var0[m], n0_var, 2 * (i + 1) + m, n0_rstd)

            for s in range(2):
                rsqrt(rstd0[s], var0[s], n0_var, s, n0_rstd)
            over_pairs(pool, step)

        @block.vector
        def _(dve):
            def add_x(i, s):
                n = 2 * i + s
                dve.wait_ge(h_in[s], 32 * (i + 1))
                nc.vector.tensor_tensor(hin[s][:, :, :], hin[s][:, :, :], xin[s][:, :, :], ALU.add).then_inc(x1_done, 1)

            def in_moments(i, s):
                n = 2 * i + s
                dve.wait_ge(x1_done, n + 1)
                moments(nc, dve, [hin[s][:, b, :] for b in range(NB)], stats0[s], mom0[s], var0[s][:, :, 0], n0_stats, n0_mom, n0_var, n)

            def norm_in(i, s):
                n = 2 * i + s
                dve.wait_ge(n0_rstd, n + 1)
                dve.wait_ge(n0_mom, 6 * n + 6)
                for b in range(NB):
                    last = nc.vector.tensor_scalar(normed[s][:, b, :], hin[s][:, b, :], mom0[s][:, 5, b:b + 1], rstd0[s][:, b, :], ALU.subtract, ALU.mult)
                last.then_inc(n0_done, 1)

            def split_h(i, s, m):
                n = turn_of(i, s, m)
                for kd in range(KD):
                    if m == 0:
                        dve.wait_ge(in_copied, 2 * (2 * i + s) + kd + 1)
                    else:
                        dve.wait_ge(h_added, 2 * turn_of(i, s, m - 1) + kd + 1)
                    nc.vector.tensor_copy(hhi[s][:, kd, :], hT[s][:, kd, :]).then_inc(h_hi, 1)
                for kd in range(KD):
                    dve.wait_ge(h_hi, 2 * n + kd + 1)
                    nc.vector.tensor_tensor(hlo[s][:, kd, :], hT[s][:, kd, :], hhi[s][:, kd, :].bitcast(F32), ALU.subtract).then_inc(h_lo, 1)

            def block_stats(i, s, m):
                n = turn_of(i, s, m)

                def ready(b):
                    if b % 2 == 0:
                        dve.wait_ge(first_done, 2 * n + b // 2 + 1)

                moments(nc, dve, [lin[s][b // 2][:, (b % 2) * DM:(b % 2 + 1) * DM] for b in range(NB)], stats[s], mom[s], var[s][:, :, 0],
                        b_stats, b_mom, b_var, n, sign=-1, ready=ready)

            def rest_g(i, s, m):
                n = turn_of(i, s, m)
                for kd in range(KD):
                    dve.wait_ge(g_hi, 2 * n + kd + 1)
                    nc.vector.tensor_tensor(glo[s][:, kd, :], g[s][:, kd, :], ghi[s][:, kd, :].bitcast(F32), ALU.subtract).then_inc(g_lo, 1)

            def add_h(i, s, m):
                n = turn_of(i, s, m)
                for kd in range(KD):
                    dve.wait_ge(second_done, 2 * n + kd + 1)
                    nc.vector.scalar_tensor_tensor(hT[s][:, kd, :], lin[s][kd][:, :], bias[:, m, kd:kd + 1], hT[s][:, kd, :], ALU.add, ALU.add).then_inc(h_added, 1)

            def add_out(i, s):
                n = 2 * i + s
                dve.wait_ge(x_saved, n + 1)
                wait(dve, stored[s], 16 * i)
                for j in range(2):
                    dve.wait_ge(out_turned, 2 * n + j + 1)
                    nc.vector.tensor_tensor(outb[s][:, 2 * j:2 * j + 2, :], lin[s][j][:, :].rearrange("p (b d) -> p b d", b=2),
                                            x1[s][:, 2 * j:2 * j + 2, :], ALU.add).then_inc(out_added, 1)

            prepare_next = [lambda i: add_x(i, 0), lambda i: in_moments(i, 0), lambda i: add_x(i, 1), lambda i: in_moments(i, 1),
                            lambda i: norm_in(i, 0), lambda i: norm_in(i, 1)]

            def step(i):
                for m in range(BLOCKS):
                    block_stats(i, 0, m)
                    if m > 0:
                        add_h(i, 1, m - 1)
                    elif precedes_pair(i):
                        add_h(i - 1, 1, BLOCKS - 1)
                        add_out(i - 1, 1)
                    split_h(i, 1, m)
                    if follows_pair(i):
                        prepare_next[2 * m](i + 1)
                    rest_g(i, 0, m)
                    block_stats(i, 1, m)
                    add_h(i, 0, m)
                    if m + 1 < BLOCKS:
                        split_h(i, 0, m + 1)
                    if follows_pair(i):
                        prepare_next[2 * m + 1](i + 1)
                    if m == BLOCKS - 1:
                        add_out(i, 0)
                        if follows_pair(i):
                            split_h(i + 1, 0, 0)
                    rest_g(i, 1, m)

            for s in range(2):
                add_x(0, s)
                in_moments(0, s)
            for s in range(2):
                norm_in(0, s)
            split_h(0, 0, 0)
            over_pairs(dve, step)
            add_h(PAIRS - 1, 1, BLOCKS - 1)
            add_out(PAIRS - 1, 1)


OUTPUT = ((SEQ, LEN, DM), "float32")


def program(nc, x, out, w):
    h = [nc.dram_tensor(f"h{i}", [SEQ, LEN, DM], F32, kind="Internal").ap() for i in range(2)]
    for phase in (
            lambda: mamba_layers(nc, x, h[0], h[1], w),
            lambda: mlp(nc, h[1], x, out, w)):
        with nc.cleanup_on_exit():
            phase()


def laid_out(inputs):
    spread = np.zeros((DM // QGROUP, DM), np.float32)
    spread[np.arange(DM) // QGROUP, np.arange(DM)] = 1
    rowsel = np.zeros((PARTS * 32, P), np.float32)
    rowsel[::32] = 1
    a = {n.split("_", 2)[2]: np.asarray(v) for n, v in inputs.items()}

    def swap(v):
        return v.transpose(0, 2, 1)

    def columns(v, rows=P):
        return swap(v.reshape(v.shape[0], -1, rows))

    def taps(v):
        return v.reshape(LAYERS, QCONV, P, TAPS).transpose(0, 2, 1, 3).reshape(LAYERS, P, QCONV * TAPS)

    def rows(v):
        return np.broadcast_to(v[:, None, :], (LAYERS, P, v.shape[1]))

    def heads(v):
        return np.repeat(columns(v, 2), HD, axis=1)

    vectors = {"ln_w": columns(a["ln_w"]), "ln_b": columns(a["ln_b"]), "rms_w": columns(a["rms_w"]), "conv_w": taps(a["conv_w"]),
               "conv_b": columns(a["conv_b"]), "dt_bias": rows(a["dt_bias"]), "A_log": rows(a["A_log"]), "D": heads(a["D"])}
    arrays = {
        "x": a["x"], "vectors": np.concatenate([vectors[n] for n in VECTORS], axis=2).transpose(1, 0, 2),
        "in_proj": swap(a["in_proj_w"]), "out_proj": swap(a["out_proj_w"]),
        "qweights": swap(a["qweights"]), "scales": swap(a["scales"]), "biases": a["biases"],
        "lora_a": a["lora_a"], "lora_b": swap(a["lora_b"]), "gamma": columns(a["ln_gamma"]), "beta": columns(a["ln_beta"]),
        "bias_columns": columns(a["biases"]),
        "constants": constants(), "spread": spread, "rowsel": rowsel,
    }
    return {f"in_{n}": np.ascontiguousarray(v) for n, v in arrays.items()}


def kernel(**inputs):
    import concourse.bacc as bacc
    from concourse.bass_utils import run_bass_kernel_spmd

    arrays = laid_out(inputs)
    nc = bacc.Bacc("TRN2", target_bir_lowering=False, num_devices=1)
    w = {n[3:]: nc.dram_tensor(n, v.shape, mybir.dt.from_np(v.dtype), kind="ExternalInput").ap() for n, v in arrays.items()}
    out = nc.dram_tensor("out", OUTPUT[0], F32, kind="ExternalOutput").ap()
    program(nc, w["x"], out, w)
    result = run_bass_kernel_spmd(nc, [arrays], core_ids=[0])
    return result.results[0]["out"]
```
